# Optimizing a Trainium2 kernel written in Bass

```python
import numpy as np
import jax
import jax.numpy as jnp

def _softmax(x, axis=-1):
    return jax.nn.softmax(x, axis=axis)

def _gelu(x):
    return jax.nn.gelu(x, approximate=True)

def _silu(x):
    return jax.nn.silu(x)

def _sigmoid(x):
    return jax.nn.sigmoid(x)

def _layernorm(x, axis=-1, eps=1e-05):
    m = jnp.mean(x, axis=axis, keepdims=True)
    v = jnp.var(x, axis=axis, keepdims=True)
    return (x - m) / jnp.sqrt(v + eps)

def _scatter_add(tgt, idx, src, axis=0):
    return tgt.at[idx].add(src)

def _segment_sum(src, seg, n):
    return jax.ops.segment_sum(src, seg, n)
kernel_name = 'mk_xattn_ffn_d1_seqx_r4_88eaef'

def setup_inputs(seed: int=0):
    np.random.seed(seed)
    _w = jnp.asarray

    def _rec_inputs():
        import jax
        import jax.numpy as jnp
        _rk = jax.random.key(seed)
        x = 7.22e-05 + 1 * jax.random.normal(jax.random.fold_in(_rk, 1), (4, 1024, 256), jnp.float32)
        _lenS = 1024 - jax.random.randint(jax.random.fold_in(_rk, 7), (4,), 0, max(1, 1024 // 4) + 1, jnp.int32)
        _lenS2 = 77 - jax.random.randint(jax.random.fold_in(_rk, 8), (4,), 0, max(1, 77 // 4) + 1, jnp.int32)
        _ctx_1024P = jax.random.normal(jax.random.fold_in(_rk, 11), (4, 16, 256), jnp.float32)
        _ctx_1024c = jax.random.dirichlet(jax.random.fold_in(_rk, 511), 0.3 * jnp.ones((16,), jnp.float32), (4, 77))
        _ctx_1024t = jnp.einsum('bsk,bkd->bsd', _ctx_1024c, _ctx_1024P)
        _ctx_1024t = _ctx_1024t * jax.lax.rsqrt(jnp.mean(jnp.square(_ctx_1024t)) + 1e-12) * 0.953939
        ctx_1024 = 4.13588e-05 + 0.999923 * (_ctx_1024t + 0.3 * jax.random.normal(jax.random.fold_in(_rk, 611), (4, 77, 256), jnp.float32))
        return (x, ctx_1024)
    x, ctx_1024 = _rec_inputs()

    def _L0_xattn_setup():
        import jax, jax.numpy as jnp
        import numpy as np
        D_MODEL = 256
        N_HEADS = 16
        HEAD_DIM = D_MODEL // N_HEADS
        SCALE = HEAD_DIM ** (-0.5)
        key = jax.random.key(seed)
        ks = jax.random.split(key, 11)
        B, L = (4, 512)
        s = 1.0 / np.sqrt(D_MODEL)
        inp = {'queries': jax.random.normal(ks[0], (B, L, D_MODEL), jnp.float32), 'keys': jax.random.normal(ks[1], (B, L, D_MODEL), jnp.float32), 'values': jax.random.normal(ks[2], (B, L, D_MODEL), jnp.float32), 'Wq': jax.random.normal(ks[3], (D_MODEL, D_MODEL), jnp.float32) * s, 'bq': jnp.zeros((D_MODEL,), jnp.float32), 'Wk': jax.random.normal(ks[4], (D_MODEL, D_MODEL), jnp.float32) * s, 'bk': jnp.zeros((D_MODEL,), jnp.float32), 'Wv': jax.random.normal(ks[5], (D_MODEL, D_MODEL), jnp.float32) * s, 'bv': jnp.zeros((D_MODEL,), jnp.float32), 'Wo': jax.random.normal(ks[6], (D_MODEL, D_MODEL), jnp.float32) * s, 'bo': jnp.zeros((D_MODEL,), jnp.float32)}
        return inp
    _L0_xattn_all = _L0_xattn_setup()
    _L0_xattn_in = {k: v for k, v in _L0_xattn_all.items() if k in ('Wq', 'bq', 'Wk', 'bk', 'Wv', 'bv', 'Wo', 'bo')}
    del _L0_xattn_all

    def _L0_ffn_setup():
        import math
        import jax, jax.numpy as jnp
        import numpy as np
        B, S, D, H, E, K = (4, 512, 256, 1024, 8, 2)
        CAPACITY_RATIO = 1.05
        key = jax.random.key(seed)
        k0, k1, k2, k3 = jax.random.split(key, 4)
        x = jax.random.normal(k0, (B, S, D), jnp.float32)
        Wg = jax.random.normal(k1, (D, E), jnp.float32) * 0.02
        W1 = jax.random.normal(k2, (E, D, H), jnp.float32) * 0.02
        b1 = jnp.zeros((E, H), jnp.float32)
        W2 = jax.random.normal(k3, (E, H, D), jnp.float32) * 0.02
        b2 = jnp.zeros((E, D), jnp.float32)
        return {'x': x, 'Wg': Wg, 'W1': W1, 'b1': b1, 'W2': W2, 'b2': b2}
    _L0_ffn_all = _L0_ffn_setup()
    _L0_ffn_in = {k: v for k, v in _L0_ffn_all.items() if k in ('Wg', 'W1', 'b1', 'W2', 'b2')}
    del _L0_ffn_all
    return {'x': x, 'ctx_1024': ctx_1024, 'L0_xattn_Wq': _L0_xattn_in['Wq'], 'L0_xattn_bq': _L0_xattn_in['bq'], 'L0_xattn_Wk': _L0_xattn_in['Wk'], 'L0_xattn_bk': _L0_xattn_in['bk'], 'L0_xattn_Wv': _L0_xattn_in['Wv'], 'L0_xattn_bv': _L0_xattn_in['bv'], 'L0_xattn_Wo': _L0_xattn_in['Wo'], 'L0_xattn_bo': _L0_xattn_in['bo'], 'L0_ffn_Wg': _L0_ffn_in['Wg'], 'L0_ffn_W1': _L0_ffn_in['W1'], 'L0_ffn_b1': _L0_ffn_in['b1'], 'L0_ffn_W2': _L0_ffn_in['W2'], 'L0_ffn_b2': _L0_ffn_in['b2']}

def reference(x, ctx_1024, L0_xattn_Wq, L0_xattn_bq, L0_xattn_Wk, L0_xattn_bk, L0_xattn_Wv, L0_xattn_bv, L0_xattn_Wo, L0_xattn_bo, L0_ffn_Wg, L0_ffn_W1, L0_ffn_b1, L0_ffn_W2, L0_ffn_b2):
    import jax
    import jax.numpy as jnp

    def _L0_xattn_ref(queries, keys, values, Wq, bq, Wk, bk, Wv, bv, Wo, bo):
        import jax, jax.numpy as jnp
        import numpy as np
        D_MODEL = 256
        N_HEADS = 16
        HEAD_DIM = D_MODEL // N_HEADS
        SCALE = HEAD_DIM ** (-0.5)
        B, L, _ = queries.shape
        S = keys.shape[1]
        q = (queries @ Wq + bq).reshape(B, L, N_HEADS, HEAD_DIM).transpose(0, 2, 1, 3)
        k = (keys @ Wk + bk).reshape(B, S, N_HEADS, HEAD_DIM).transpose(0, 2, 1, 3)
        v = (values @ Wv + bv).reshape(B, S, N_HEADS, HEAD_DIM).transpose(0, 2, 1, 3)
        scores = jnp.einsum('bhld,bhsd->bhls', q, k) * SCALE
        weights = jax.nn.softmax(scores, axis=-1)
        out = jnp.einsum('bhls,bhsd->bhld', weights, v)
        out = out.transpose(0, 2, 1, 3).reshape(B, L, D_MODEL)
        out = out @ Wo + bo
        return out

    def _L0_ffn_ref(x, Wg, W1, b1, W2, b2):
        import math
        import jax, jax.numpy as jnp
        import numpy as np
        B, S, D, H, E, K = (4, 512, 256, 1024, 8, 2)
        CAPACITY_RATIO = 1.05
        b, s, d = x.shape
        e = Wg.shape[1]
        n = b * s
        cap = int(math.ceil(n * K / e * CAPACITY_RATIO))
        xf = x.reshape(n, d)
        probs = jax.nn.softmax(xf @ Wg, axis=-1)
        topv, topi = jax.lax.top_k(probs, K)
        gates = topv / jnp.sum(topv, axis=-1, keepdims=True)
        eidx = topi.reshape(-1)
        oh = jax.nn.one_hot(eidx, e, dtype=jnp.int32)
        pos = jnp.sum(jnp.cumsum(oh, axis=0) * oh, axis=-1) - 1
        keep = pos < cap
        dest = jnp.where(keep, eidx * cap + pos, e * cap)
        xr = jnp.repeat(xf, K, axis=0)
        buf = jnp.zeros((e * cap + 1, d), x.dtype).at[dest].set(xr)
        expert_in = buf[:e * cap].reshape(e, cap, d)
        h = jax.nn.gelu(jnp.einsum('ecd,edh->ech', expert_in, W1) + b1[:, None, :])
        y = jnp.einsum('ech,ehd->ecd', h, W2) + b2[:, None, :]
        yf = jnp.concatenate([y.reshape(e * cap, d), jnp.zeros((1, d), y.dtype)], axis=0)
        gathered = yf[dest]
        w = (gates.reshape(-1) * keep.astype(gates.dtype))[:, None]
        out = (gathered * w).reshape(n, K, d).sum(axis=1).reshape(b, s, d)
        return out
    x = x + _L0_xattn_ref(_layernorm(x, axis=-1), ctx_1024, ctx_1024, L0_xattn_Wq, L0_xattn_bq, L0_xattn_Wk, L0_xattn_bk, L0_xattn_Wv, L0_xattn_bv, L0_xattn_Wo, L0_xattn_bo)
    x = x + _L0_ffn_ref(_layernorm(x, axis=-1), L0_ffn_Wg, L0_ffn_W1, L0_ffn_b1, L0_ffn_W2, L0_ffn_b2)
    return x

_drawn_inputs = setup_inputs


def setup_inputs(seed=0):
    import zlib

    import numpy as np

    out = dict(_drawn_inputs(seed))
    spreads = {'L0_xattn_bq': (0.0, 0.289),
     'L0_xattn_bk': (0.0, 0.8),
     'L0_xattn_bv': (0.0, 0.1),
     'L0_xattn_bo': (0.0, 0.1),
     'L0_ffn_b1': (0.0, 0.359),
     'L0_ffn_b2': (0.0, 0.1)}
    factors = {}
    for name, (base, spread) in spreads.items():
        noise = np.random.default_rng([zlib.crc32(name.encode()), seed]).standard_normal(out[name].shape)
        drawn = base * np.exp(spread * noise) if base else spread * noise
        out[name] = jnp.asarray(drawn.astype(out[name].dtype))
    for name, factor in factors.items():
        out[name] = (out[name] * factor).astype(out[name].dtype)
    return out
```

```python
from contextlib import ExitStack

import concourse.bass as bass
from concourse import mybir
from concourse.alu_op_type import AluOpType as ALU

F32 = mybir.dt.float32
F32R = mybir.dt.float32r
BF16 = mybir.dt.bfloat16
I32 = mybir.dt.int32
U32 = mybir.dt.uint32
ACT = mybir.ActivationFunctionType
AX_X = mybir.AxisListType.X

P = 128
B, L, D = 4, 1024, 256
S, H = 77, 16
HD = D // H
SCALE = HD ** -0.5
EPS = 1e-5
E, HID, TOPK = 8, 1024, 2
NTOK = B * L
CAP = -(-NTOK * TOPK * 105 // (E * 100))
CH = 512
NCH = NTOK // CH
SUB = CH // P
KC = D // P
GH = 4
NG = H // GH
GROWS = GH * S
TL = [104, 102, 102]
TO = [0, 104, 206]
TW = max(TL)
NT = NG * len(TL)
TT = 120
XC = 3 * TT
NX = -(-CAP // XC)
ROW = D + 1 + E
BIG = 100000.0
KROWS = 3 * 2 * HD + H


T_XT, T_Q, T_MAX, T_NEGMAX = 1, 3, 5, 9
T_RECIP, T_SPREAD, T_OT, T_WO, T_X2T, T_LOGITS = 2, 4, 5, 8, 10, 11


def segments():
    out = []
    for hl in range(GH):
        for j in range(len(TL)):
            lo, hi = max(hl * S, TO[j]), min((hl + 1) * S, TO[j] + TL[j])
            if lo < hi:
                out.append((hl, j, lo - TO[j], lo - hl * S, hi - lo))
    return out


C_ID = 0
C_TRI = C_ID + P
C_SEL = C_TRI + P
C_BLK = C_SEL + 2 * P
C_VM = C_BLK + 8 * S
C_ON = C_VM + 3 * 64
C_OH = C_ON + 3 * 64
C_IO = C_OH + NT * TW
C_EB = C_IO + SUB * E
C_N = C_EB + SUB * E


def constants(np):
    c = np.zeros((P, C_N), np.float32)
    c[:, C_ID:C_ID + P] = np.eye(P)
    c[:, C_TRI:C_TRI + P] = np.triu(np.ones((P, P)), 1)
    for g in range(NG):
        for hl in range(GH):
            at = C_SEL + (g // 2) * P + 64 * (g % 2) + HD * hl
            c[32 * g + 8 * hl, at:at + HD] = 1
    for h in range(8):
        c[HD * h:HD * h + HD, C_BLK + S * h:C_BLK + S * h + S] = 1
    for hl, j, p0, _, n in segments():
        c[p0:p0 + n, C_VM + 64 * j + HD * hl:C_VM + 64 * j + HD * hl + HD] = 1
        c[p0:p0 + n, C_ON + 64 * j + 8 * hl:C_ON + 64 * j + 8 * hl + 8] = 1
        for g in range(NG):
            t = 3 * g + j
            c[96 + GH * g + hl, C_OH + TW * t + p0:C_OH + TW * t + p0 + n] = 1
    c[:, C_IO:C_IO + 32] = np.tile(np.arange(8), 4)
    c[:, C_EB:C_EB + 32] = np.tile(np.arange(8) * CAP, 4)
    return c


COUNTS = """xn_stats xn_mv xn_ve xn_rs xn_ready xt_psum xt_hi xt_lo q_psum q_hi q_lo max_psum max_read negmax
    nmt_psum nmt_ready sc_psum p_hi p_full p_lo pv_tile pv_group ou_ready dt_ready rd_ready rd_hi rd_lo
    rb_psum ot_ready ot_hi ot_lo wo_psum xr_bias x1_ready x1_stored x2_stats x2_mv x2_ve x2_rs x2_ready
    tok_ready x2t_psum x2t_ready lg_psum lg_ready top_ready idx_ready idf_ready dif_ready ex_ready
    den_ready gate0 gate1 oh_ready gw_ready both_ready bothb_ready carry_ready carryb_ready pos_psum
    pos_a pos_b pos_c pk_ready destf_ready dest_ready tok_row x_loaded xr_loaded kbm_loaded k_loaded
    vh_loaded vl_loaded v_masked half_ready""".split()
EXPERT_COUNTS = """w_high w_split b1_loaded xt_psum xt_high xt_low h_psum h_high h_full h_low l2_done
    y_psum b2g_ready y_ready""".split()


def prime(eng, semaphores):
    for one in semaphores:
        eng.sem_inc(one, 1)


def wait(eng, sem, count, primed=1):
    if not isinstance(count, int) or count > 0:
        eng.wait_ge(sem, count + primed)


def wait_apart(eng, passed, sem, count):
    wait(eng, sem, count)
    eng.sem_inc(passed, 1)


def build(nc, x, ctxT, watt, wg, bcols, brows, w1, b1, w2, b2, cst, out):
    slots = nc.dram_tensor("slots", (E * CAP, ROW), F32, kind="Internal").ap()
    with ExitStack() as top:
        sb = lambda name, shape, dt: top.enter_context(nc.sbuf_tensor(name, shape, dt))
        sem = lambda name: top.enter_context(nc.semaphore(name))
        whole = dict(
            cc=sb("cc", [P, C_N], F32), s_init=sem("s_init"), s_scat=sem("s_scat"),
            s={n: sem("s_" + n) for n in COUNTS}, q_stacked=[sem(f"s_q_stacked{u}") for u in range(2)],
            e={n: sem("e_" + n) for n in EXPERT_COUNTS}, s_w=sem("e_weights"),
            x_in=[sem(f"e_x_in{i}") for i in range(NX)], added=[sem(f"e_added{i}") for i in range(NX)])
        passed = {n: sem("passed_" + n) for n in ("act", "dve", "pool")}
        banks = [top.enter_context(nc.psum_tensor(f"bank{i}", [P, 512], F32)) for i in range(8)]
        with ExitStack() as att:
            attention_and_routing(nc, att, whole, passed, banks, slots, x, ctxT, watt, wg, bcols, brows, cst, out)
        with ExitStack() as ffn:
            experts(nc, ffn, whole, passed, banks, slots, w1, b1, w2, b2, out)


def attention_and_routing(nc, ctx, whole, passed, banks, slots, x, ctxT, watt, wg, bcols, brows, cst, out):
    sb = lambda name, shape, dt: ctx.enter_context(nc.sbuf_tensor(name, shape, dt))
    sem = lambda name: ctx.enter_context(nc.semaphore(name))
    cc = whole["cc"]
    s_init, s_scat = whole["s_init"], whole["s_scat"]
    ident = cc[:, C_ID:C_ID + P]
    blk = cc[:, C_BLK:C_BLK + 616].rearrange("p (h s) -> p h s", h=8)

    wh = sb("wh", [P, 2, KC, D], F32R)
    wl = sb("wl", [P, 2, KC, D], F32R)
    wgs = sb("wgs", [P, KC, E], F32)
    bc = sb("bc", [P, 2, KC], F32)
    bo_row = sb("bo_row", [P, D], F32)
    k_parts = nc.dram_tensor("k_parts", (2, B, P, 2, 8 * S), F32, kind="Internal").ap()
    v_parts = nc.dram_tensor("v_parts", (2, B, S, D), F32, kind="Internal").ap()
    tri = sb("tri", [P, P], BF16)
    ones = sb("ones", [P, P], BF16)
    selr = sb("selr", [P, 2, P], F32R)
    kst = sb("kst", [KROWS, NT, TW], F32R)
    vraw_h = sb("vraw_h", [TW, NT, 64], F32R)
    vraw_l = sb("vraw_l", [TW, NT, 64], F32R)
    vsth = sb("vsth", [TW, NT, P], F32R)
    vstl = sb("vstl", [TW, NT, P], F32R)

    with ExitStack() as pre:
        psb = lambda name, shape, dt: pre.enter_context(nc.sbuf_tensor(name, shape, dt))
        psem = lambda name: pre.enter_context(nc.semaphore(name))
        wraw = psb("wraw", [P, 4, KC, D], F32)
        kbh = psb("kbh", [P, B, 2, 8 * S], F32R)
        kbl = psb("kbl", [P, B, 2, 8 * S], F32R)
        vh = psb("vh", [S, B, D], F32R)
        vl = psb("vl", [S, B, D], F32R)
        wkvh = psb("wkvh", [P, 2, KC, D], F32R)
        wkvl = psb("wkvl", [P, 2, KC, D], F32R)
        craw = psb("craw", [P, KC, B * S], F32)
        ch = psb("ch", [P, KC, B * S], F32R)
        cl = psb("cl", [P, KC, B * S], F32R)
        bv_row = psb("bv_row", [P, D], F32)
        kf = psb("kf", [P, 2, B * S], F32)
        kh = psb("kh", [P, 2, B * S], F32R)
        kl = psb("kl", [P, 2, B * S], F32R)
        vf = psb("vf", [S, B, D], F32)
        fill = psb("fill", [P, ROW], F32)
        s_load, s_cst, s_wl, s_cl, s_pre = (psem(n) for n in ("s_load", "s_cst", "s_wl", "s_cl", "s_pre"))
        s_k, s_v, s_kf, s_kh, s_kl, s_vf, s_fill, s_kb, s_kbh, s_kept = (
            psem(n) for n in ("s_k", "s_v", "s_kf", "s_kh", "s_kl", "s_vf", "s_fill", "s_kb", "s_kbh", "s_kept"))
        block = pre.enter_context(nc.Block())

        @block.sync
        def _(sp):
            for group in (whole["s"].values(), whole["q_stacked"], whole["e"].values(),
                          [whole["s_w"]], whole["x_in"]):
                prime(sp, group)
            sp.dma_start(craw[:], ctxT).then_inc(s_load, 16)
            sp.dma_start(wraw[:], watt).then_inc(s_load, 16)
            sp.dma_start(bc[:], bcols).then_inc(s_load, 16)
            sp.dma_start(bv_row[:], brows[0:1, :].to_broadcast([P, D])).then_inc(s_load, 16)
            sp.dma_start(bo_row[:], brows[1:2, :].to_broadcast([P, D])).then_inc(s_load, 16)
            sp.dma_start(wgs[:], wg).then_inc(s_load, 16)
            sp.dma_start(cc[:], cst).then_inc(s_cst, 16)
            sp.wait_ge(s_fill, 2)
            n = E * CAP // P
            sp.dma_start(slots[0:n * P, :].rearrange("(n p) r -> p n r", p=P),
                         fill[:].rearrange("p (a r) -> p a r", a=1).to_broadcast([P, n, ROW])).then_inc(s_init, 16)
            sp.wait_ge(s_vf, B + 2)
            for r, part in enumerate((vh, vl)):
                sp.dma_start(v_parts[r].rearrange("b s d -> s b d"), part[:].bitcast(F32)).then_inc(s_kept, 16)
            sp.wait_ge(s_kbh, 2 * B)
            sp.dma_start(k_parts[0].rearrange("b p m c -> p b m c"), kbh[:].bitcast(F32)).then_inc(s_kept, 16)
            sp.wait_ge(s_kb, 2 * B)
            sp.dma_start(k_parts[1].rearrange("b p m c -> p b m c"), kbl[:].bitcast(F32)).then_inc(s_kept, 16)
            sp.wait_ge(s_kept, 64)
            sp.wait_ge(s_init, 16)

        @block.gpsimd
        def _(pool):
            pool.memset(fill[:], 0.0).then_inc(s_fill, 1)
            pool.wait_ge(s_fill, 1)
            pool.memset(fill[:].bitcast(I32)[:, D:D + 1], int(BIG)).then_inc(s_fill, 1)
            pool.wait_ge(s_fill, 2)
            done = E * CAP // P * P
            pool.dma_start(slots[done:E * CAP, :], fill[0:E * CAP - done, :]).then_inc(s_scat, 16)
            pool.wait_ge(s_scat, 16)
            for raw in (vraw_h, vraw_l):
                pool.memset(raw[:].bitcast(F32), 0.0).then_inc(s_pre, 1)
            pool.memset(vstl[:, :, 64:P].bitcast(F32), 0.0).then_inc(s_pre, 1)
            pool.wait_ge(s_cst, 16)
            pool.wait_ge(s_kl, 1)
            for b in range(B):
                for m in range(2):
                    pool.tensor_tensor(kbl[:, b, m, :].rearrange("p (h s) -> p h s", h=8),
                                       kl[:, m, b * S:b * S + S].rearrange("p (a s) -> p a s", a=1).to_broadcast([P, 8, S]),
                                       blk, ALU.mult).then_inc(s_kb, 1)

        @block.scalar
        def _(act):
            act.wait_ge(s_cst, 16)
            act.activation(kst[96:112, :, :], cc[96:112, C_OH:C_OH + NT * TW].rearrange("p (t w) -> p t w", t=NT),
                           ACT.Copy).then_inc(s_pre, 1)
            act.activation(selr[:], cc[:, C_SEL:C_SEL + 256].rearrange("p (k m) -> p k m", k=2),
                           ACT.Copy).then_inc(s_pre, 1)
            act.activation(tri[:], cc[:, C_TRI:C_TRI + P], ACT.Copy).then_inc(s_pre, 1)
            for g in range(NG):
                act.activation(vsth[:, 3 * g:3 * g + 3, 64:P],
                               cc[0:TW, C_ON:C_ON + 192].rearrange("p (j w) -> p j w", j=3),
                               ACT.Copy).then_inc(s_pre, 1)

        @block.tensor
        def _(pe):
            pe.wait_ge(s_wl, 4)
            pe.wait_ge(s_cl, 2)
            for m in range(2):
                n = 0
                for a, c in ((wkvh, ch), (wkvh, cl), (wkvl, ch)):
                    for kc in range(KC):
                        mm = pe.matmul(banks[m][:, 0:B * S], a[:, 0, kc, P * m:P * m + P], c[:, kc, :],
                                       start=(n == 0), stop=(n == 5))
                        n += 1
                mm.then_inc(s_k, 1)
            for b in range(B):
                n = 0
                for c, a in ((ch, wkvh), (ch, wkvl), (cl, wkvh)):
                    for kc in range(KC):
                        mm = pe.matmul(banks[2 + b][0:S, 0:D], c[:, kc, b * S:b * S + S], a[:, 1, kc, :],
                                       start=(n == 0), stop=(n == 5))
                        n += 1
                mm.then_inc(s_v, 1)

        @block.vector
        def _(dve):
            dve.memset(ones[:], 1.0).then_inc(s_pre, 1)
            dve.wait_ge(s_load, 96)
            dve.tensor_copy(ch[:], craw[:]).then_inc(s_cl, 1)
            dve.wait_ge(s_cl, 1)
            dve.tensor_tensor(cl[:], craw[:], ch[:], ALU.subtract).then_inc(s_cl, 1)
            dve.tensor_copy(wkvh[:], wraw[:, 0:2]).then_inc(s_wl, 1)
            dve.tensor_copy(wh[:], wraw[:, 2:4]).then_inc(s_wl, 1)
            dve.wait_ge(s_wl, 2)
            dve.tensor_tensor(wkvl[:], wraw[:, 0:2], wkvh[:], ALU.subtract).then_inc(s_wl, 1)
            dve.tensor_tensor(wl[:], wraw[:, 2:4], wh[:], ALU.subtract).then_inc(s_wl, 1)
            for m in range(2):
                dve.wait_ge(s_k, m + 1)
                dve.tensor_scalar(kf[:, m, :], banks[m][:, 0:B * S], bc[:, 1, m:m + 1], None, ALU.add).then_inc(s_kf, 1)
            dve.wait_ge(s_kf, 2)
            dve.tensor_copy(kh[:], kf[:]).then_inc(s_kh, 1)
            dve.wait_ge(s_kh, 1)
            dve.tensor_tensor(kl[:], kf[:], kh[:], ALU.subtract).then_inc(s_kl, 1)
            for b in range(B):
                dve.wait_ge(s_v, b + 1)
                dve.tensor_tensor(vf[:, b, :], banks[2 + b][0:S, 0:D], bv_row[0:S, :], ALU.add).then_inc(s_vf, 1)
            dve.wait_ge(s_vf, B)
            dve.tensor_copy(vh[:], vf[:]).then_inc(s_vf, 1)
            dve.wait_ge(s_vf, B + 1)
            dve.tensor_tensor(vl[:], vf[:], vh[:], ALU.subtract).then_inc(s_vf, 1)
            dve.wait_ge(s_cst, 16)
            for b in range(B):
                for m in range(2):
                    dve.tensor_tensor(kbh[:, b, m, :].rearrange("p (h s) -> p h s", h=8),
                                      kh[:, m, b * S:b * S + S].rearrange("p (a s) -> p a s", a=1).to_broadcast([P, 8, S]),
                                      blk, ALU.mult).then_inc(s_kbh, 1)

    kbm = sb("kbm", [P, 2, 8 * S], F32R)
    xt = sb("xt", [P, SUB, D], F32)
    xr = sb("xr", [P, SUB, D], F32)
    st = sb("st", [P, SUB, 6], F32)
    mv = sb("mv", [P, SUB, 2], F32)
    ve = sb("ve", [P, SUB], F32)
    rs = sb("rs", [P, SUB], F32)
    half = sb("half", [P, SUB], F32)
    xn = sb("xn", [P, SUB, D], F32)
    xth = sb("xth", [P, KC, CH], F32R)
    xtl = sb("xtl", [P, KC, CH], F32R)
    qh = sb("qh", [P, 2, CH], F32R)
    ql = sb("ql", [P, 2, CH], F32R)
    mx = sb("mx", [P, SUB, H], F32)
    nm = sb("nm", [P, SUB, H], F32)
    nmt = sb("nmt", [H, CH], F32R)
    qs = sb("qs", [KROWS, 2, NT, CH], F32R)
    NP = 3
    pf = sb("pf", [TW, NP, CH], F32)
    ph = sb("ph", [TW, NP, CH], F32R)
    pl = sb("pl", [TW, NP, CH], F32R)
    ou = sb("ou", [P, 2, CH], F32)
    dt = sb("dt", [P, CH], F32)
    rd = sb("rd", [P, CH], F32)
    rdh = sb("rdh", [P, CH], F32R)
    rdl = sb("rdl", [P, CH], F32R)
    ot = sb("ot", [P, 2, CH], F32)
    oth = sb("oth", [P, 2, CH], F32R)
    otl = sb("otl", [P, 2, CH], F32R)
    x1 = sb("x1", [P, SUB, D], F32)
    st2 = sb("st2", [P, SUB, 6], F32)
    mv2 = sb("mv2", [P, SUB, 2], F32)
    ve2 = sb("ve2", [P, SUB], F32)
    rs2 = sb("rs2", [P, SUB], F32)
    row = sb("row", [P, SUB, ROW], F32)
    x2t = sb("x2t", [P, KC, CH], F32)
    lg = sb("lg", [P, SUB, E], F32)
    top8 = sb("top8", [P, SUB, 8], F32)
    idx8 = sb("idx8", [P, SUB, 8], U32)
    idf = sb("idf", [P, SUB, TOPK], F32)
    dif = sb("dif", [P, SUB], F32)
    ex = sb("ex", [P, SUB], F32)
    den = sb("den", [P, SUB], F32)
    gate = sb("gate", [P, SUB, TOPK], F32)
    oh = sb("oh", [P, TOPK, SUB, E], F32)
    gw = sb("gw", [P, SUB, E], F32)
    gw1 = sb("gw1", [P, SUB, E], F32)
    both = sb("both", [P, SUB, E], F32)
    bothb = sb("bothb", [P, SUB, E], BF16)
    carry = sb("carry", [P, SUB + 1, E], F32)
    carryb = sb("carryb", [P, E], BF16)
    no = sb("no", [P, SUB, E], F32)
    pos = sb("pos", [P, SUB, E], F32)
    pos2 = sb("pos2", [P, SUB, E], F32)
    pk = sb("pk", [P, TOPK, SUB, E], F32)
    destf = sb("destf", [P, TOPK, SUB], F32)
    dest = sb("dest", [P, TOPK, SUB], I32)
    tok = sb("tok", [P, SUB], I32)

    s, q_stacked = whole["s"], whole["q_stacked"]
    QS = 16 * 19
    xv = x.rearrange("(c i p) d -> c p i d", i=SUB, p=P)
    ov = out.rearrange("(c i p) d -> c p i d", i=SUB, p=P)
    SC, PV = banks[4:6], banks[6:8]

    def steps(program):
        program(-1, 1, -1, True, False, False)
        program(0, 0, 0, True, True, False)
        with program.eng.Fori(0, NCH // 2 - 1) as b:
            program(2 * b + 1, 1, b, True, True, True)
            program(2 * b + 2, 0, b + 1, True, True, True)
        program(NCH - 1, 1, NCH // 2 - 1, False, True, True)
        program(NCH, 0, NCH // 2, False, False, True)

    class Program:
        def __init__(self, eng, step):
            self.eng, self.step = eng, step

        def __call__(self, *a):
            self.step(self.eng, *a)

    def bcast(ap, shape):
        return ap.to_broadcast(shape)

    with ExitStack() as main:
        block = main.enter_context(nc.Block())

        def sync_step(sp, k, u, n, a_on, b_on, f_on):
            a, j, v = k + 1, k - 1, 1 - u
            if a_on:
                wait(sp, s["xn_ready"], SUB * a)
                sp.dma_start(xt[:], xv[a]).then_inc(s["x_loaded"], 16)
                if u == 1:
                    wait(sp, s["max_psum"], SUB * NG * a)
                    sp.dma_start(kbm[:].bitcast(F32), k_parts[0, n + 1]).then_inc(s["kbm_loaded"], 16)
            if f_on:
                wait(sp, s["x1_ready"], SUB * j)
                sp.dma_start(xr[:], xv[j]).then_inc(s["xr_loaded"], 16)
            if b_on and u == 0:
                wait(sp, s["sc_psum"], NT * k)
                for m in range(2):
                    for t in range(3):
                        lo = GROWS * m + TO[t]
                        for r, src in ((0, k_parts[0]), (32, k_parts[1]), (64, k_parts[0])):
                            p0 = 64 * m + HD * t
                            sp.dma_start(kst[r:r + 32, 3 * m + t:NT:6, 0:TL[t]].bitcast(F32),
                                         src[n, p0:p0 + 32, :, lo:lo + TL[t]]).then_inc(s["k_loaded"], 16)
                wait(sp, s["v_masked"], 2 * n)
                for hl, t, p0, s0, rows in segments():
                    for dst, src, ready in ((vraw_h, v_parts[0], "vh_loaded"), (vraw_l, v_parts[1], "vl_loaded")):
                        sp.dma_start(dst[p0:p0 + rows, t:NT:3, :].bitcast(F32),
                                     src[n, s0:s0 + rows, :].rearrange("p (g w) -> p g w", g=NG)).then_inc(s[ready], 16)
            if a_on:
                wait(sp, s["q_lo"], 2 * (a + 1))
                wait(sp, s["sc_psum"], NT * (k))
                for m in range(2):
                    for t in range(3):
                        p0 = 64 * m + HD * t
                        for r, src in ((0, qh), (32, qh), (64, ql)):
                            sp.dma_start(qs[r:r + 32, v, 3 * m + t:NT:6, :].bitcast(F32),
                                         src[p0:p0 + 32, :, :].bitcast(F32)).then_inc(q_stacked[v], 16)
                wait(sp, s["nmt_ready"], a + 1)
                sp.dma_start(qs[96:112, v, :, :].bitcast(F32),
                             bcast(nmt[:].bitcast(F32).rearrange("h (a c) -> h a c", a=1), [H, NT, CH])).then_inc(q_stacked[v], 16)
            if f_on:
                wait(sp, s["x1_ready"], SUB * (j + 1))
                sp.dma_start(ov[j], x1[:]).then_inc(s["x1_stored"], 16)

        @block.sync
        def _(sp):
            steps(Program(sp, sync_step))
            wait(sp, s["x1_stored"], 16 * NCH)

        def pe_tile(pe, k, u, n, t):
            if t == 0:
                wait(pe, q_stacked[u], QS * (n + 1))
                wait(pe, s["k_loaded"], 16 * 18 * (n + 1))
            wait(pe, s["p_full"], NT * k + t - 1)
            pe.matmul(SC[t % 2][0:TL[t % 3], :], kst[:, t, 0:TL[t % 3]], qs[:, u, t, :],
                      start=True, stop=True).then_inc(s["sc_psum"], 1)

        def pe_values(pe, k, n, t):
            g, w = t // 3, TL[t % 3]
            if t % 3 == 0:
                wait(pe, s["dt_ready"], NG * k + g - 1)
            if t == 0:
                wait(pe, s["v_masked"], 2 * (n + 1))
            wait(pe, s["p_hi"], NT * k + t + 1)
            pe.matmul(PV[g % 2][:], vsth[0:w, t, :], ph[0:w, t % NP, :], start=(t % 3 == 0), stop=False)
            pe.matmul(PV[g % 2][:], vstl[0:w, t, :], ph[0:w, t % NP, :], start=False, stop=False)
            wait(pe, s["p_lo"], NT * k + t + 1)
            mm = pe.matmul(PV[g % 2][:], vsth[0:w, t, :], pl[0:w, t % NP, :], start=False, stop=(t % 3 == 2))
            mm.then_inc(s["pv_tile"], 1)

        def pe_step(pe, k, u, n, a_on, b_on, f_on):
            a, j = k + 1, k - 1
            ba = n + 1 if u == 1 else n
            for t in range(NT):
                if b_on:
                    pe_tile(pe, k, u, n, t)
                    if t >= 2:
                        pe_values(pe, k, n, t - 2)
                if a_on and t == T_XT:
                    for h in range(KC):
                        if h == 0:
                            wait(pe, s["nmt_ready"], a)
                        for i in range(SUB):
                            wait(pe, s["xn_ready"], SUB * a + i + 1)
                            mm = pe.transpose(banks[2 + h][:, P * i:P * i + P], xn[:, i, P * h:P * h + P], ident)
                        mm.then_inc(s["xt_psum"], 1)
                if f_on and t == T_SPREAD:
                    wait(pe, s["rd_lo"], j + 1)
                    wait(pe, s["pos_b"], j)
                    for m in range(2):
                        pe.matmul(banks[m][:], selr[:, m, :], rdh[:], start=True, stop=False)
                        pe.matmul(banks[m][:], selr[:, m, :], rdl[:], start=False, stop=True).then_inc(s["rb_psum"], 1)
                if a_on and t == T_Q:
                    wait(pe, s["xt_lo"], KC * (a + 1))
                    for m in range(2):
                        c = 0
                        for w_, x_ in ((wh, xth), (wh, xtl), (wl, xth)):
                            for kc in range(KC):
                                mm = pe.matmul(banks[2 + m][:], w_[:, 0, kc, P * m:P * m + P], x_[:, kc, :],
                                               start=(c == 0), stop=(c == 5))
                                c += 1
                        mm.then_inc(s["q_psum"], 1)
                if a_on and T_MAX <= t < T_MAX + SUB:
                    i = t - T_MAX
                    for g in range(NG):
                        c = NG * i + g
                        if c == 0:
                            wait(pe, s["kbm_loaded"], 16 * (ba + 1))
                        if c < 2:
                            wait(pe, s["q_lo"], 2 * (a + 1))
                        else:
                            wait(pe, s["max_read"], SUB * NG * a + c - 1)
                        pe.matmul(banks[2 + c % 2][:, 0:GROWS], qh[:, g // 2, P * i:P * i + P],
                                  kbm[:, g // 2, GROWS * (g % 2):GROWS * (g % 2) + GROWS],
                                  start=True, stop=True).then_inc(s["max_psum"], 1)
                if a_on and t == T_NEGMAX:
                    wait(pe, s["negmax"], a + 1)
                    for i in range(SUB):
                        mm = pe.transpose(banks[2][0:H, P * i:P * i + P], nm[:, i, :], ident)
                    mm.then_inc(s["nmt_psum"], 1)
                if f_on and t == T_WO:
                    wait(pe, s["ot_lo"], 2 * (j + 1))
                    for i in range(SUB):
                        c = 0
                        for o_, w_ in ((oth, wh), (oth, wl), (otl, wh)):
                            for kc in range(KC):
                                mm = pe.matmul(banks[i // 2][:, D * (i % 2):D * (i % 2) + D],
                                               o_[:, kc, P * i:P * i + P], w_[:, 1, kc, :],
                                               start=(c == 0), stop=(c == 5))
                                c += 1
                        if i % 2:
                            mm.then_inc(s["wo_psum"], 1)
                if f_on and t == T_X2T:
                    wait(pe, s["x2_ready"], SUB * (j + 1))
                    for h in range(KC):
                        for i in range(SUB):
                            mm = pe.transpose(banks[h][:, P * i:P * i + P], row[:, i, P * h:P * h + P], ident)
                        mm.then_inc(s["x2t_psum"], 1)
                if f_on and t == T_LOGITS:
                    wait(pe, s["x2t_ready"], KC * (j + 1))
                    for i in range(SUB):
                        for kc in range(KC):
                            mm = pe.matmul(banks[0][:, E * i:E * i + E], x2t[:, kc, P * i:P * i + P], wgs[:, kc, :],
                                           start=(kc == 0), stop=(kc == KC - 1))
                    mm.then_inc(s["lg_psum"], 1)
            if b_on:
                pe_values(pe, k, n, NT - 2)
                pe_values(pe, k, n, NT - 1)
            if f_on:
                wait(pe, s["bothb_ready"], j + 1)
                wait(pe, s["carryb_ready"], j + 1)
                for i in range(SUB):
                    o = banks[1][:, E * i:E * i + E]
                    mm = pe.matmul(o, tri[:], bothb[:, i, :], start=True, stop=False)
                    for before in range(i):
                        pe.matmul(o, ones[:], bothb[:, before, :], start=False, stop=False)
                    mm = pe.matmul(o, ones[:], carryb[:], start=False, stop=True)
                mm.then_inc(s["pos_psum"], 1)

        @block.tensor
        def _(pe):
            steps(Program(pe, pe_step))

        def act_group(act, k, g):
            wait(act, s["pv_tile"], NT * k + 3 * g + 3)
            wait(act, s["ot_ready"], 2 * k)
            act.activation(ou[64 * (g % 2):64 * (g % 2) + 64, g // 2, :], PV[g % 2][0:64, :], ACT.Copy)\
               .then_inc(s["ou_ready"], 1)
            wait(act, s["rd_ready"], k)
            act.activation(dt[32 * g:32 * g + 32, :], PV[g % 2][64:96, :], ACT.Copy).then_inc(s["dt_ready"], 1)

        def act_step(act, k, u, n, a_on, b_on, f_on):
            a, j, v = k + 1, k - 1, 1 - u
            for t in range(NT):
                if b_on:
                    w = TL[t % 3]
                    wait(act, s["sc_psum"], NT * k + t + 1)
                    wait(act, s["pv_tile"], NT * k + t - NP + 1)
                    act.activation(ph[0:w, t % NP, :], SC[t % 2][0:w, :], ACT.Exp, scale=SCALE).then_inc(s["p_hi"], 1)
                    wait(act, s["p_lo"], NT * k + t - NP + 1)
                    act.activation(pf[0:w, t % NP, :], SC[t % 2][0:w, :], ACT.Exp, scale=SCALE).then_inc(s["p_full"], 1)
                    if t in (5, 8, 11):
                        act_group(act, k, (t - 5) // 3)
                if a_on and t == T_XT:
                    for h in range(KC):
                        wait(act, s["xt_psum"], KC * a + h + 1)
                        wait(act, s["q_psum"], 2 * a)
                        act.activation(xth[:, h, :], banks[2 + h][:], ACT.Copy).then_inc(s["xt_hi"], 1)
                if f_on and t == T_RECIP:
                    wait(act, s["rd_ready"], j + 1)
                    wait(act, s["rb_psum"], 2 * j)
                    act.activation(rdh[:], rd[:], ACT.Copy).then_inc(s["rd_hi"], 1)
                if f_on and t == T_OT:
                    for m in range(2):
                        wait(act, s["ot_ready"], 2 * j + m + 1)
                        wait(act, s["wo_psum"], 2 * j)
                        act.activation(oth[:, m, :], ot[:, m, :], ACT.Copy).then_inc(s["ot_hi"], 1)
                if a_on and t == T_Q:
                    wait(act, s["max_psum"], SUB * NG * a)
                    wait(act, q_stacked[u], QS * (n + 1))
                    for m in range(2):
                        wait(act, s["q_psum"], 2 * a + m + 1)
                        act.activation(qh[:, m, :], banks[2 + m][:], ACT.Identity, bias=bc[:, 0, m:m + 1])\
                           .then_inc(s["q_hi"], 1)
                if a_on and t == T_NEGMAX:
                    wait(act, s["nmt_psum"], a + 1)
                    act.activation(nmt[:], banks[2][0:H, :], ACT.Copy).then_inc(s["nmt_ready"], 1)
                if f_on and t == T_X2T:
                    for h in range(KC):
                        wait(act, s["x2t_psum"], KC * j + h + 1)
                        wait(act, s["lg_psum"], j)
                        act.activation(x2t[:, h, :], banks[h][:], ACT.Copy).then_inc(s["x2t_ready"], 1)
            if b_on:
                act_group(act, k, NG - 1)
            if f_on:
                wait(act, s["dif_ready"], j + 1)
                wait(act, s["gate1"], j)
                act.activation(ex[:], dif[:], ACT.Exp).then_inc(s["ex_ready"], 1)

        @block.scalar
        def _(act):
            steps(Program(act, act_step))

        def statistics(dve, src, c, stats, moments, s_stats, s_mv, first, free):
            for i in range(SUB):
                first(i)
                wait(dve, s_mv, SUB * c)
                dve.bn_stats(stats[:, i, :], src[:, i, :]).then_inc(s_stats, 1)
            for i in range(SUB):
                if i == 0:
                    wait(dve, free, SUB * c)
                wait_apart(dve, passed["dve"], s_stats, SUB * c + i + 1)
                dve.bn_aggr(moments[:, i, :], stats[:, i, :]).then_inc(s_mv, 1)

        def dve_step(dve, k, u, n, a_on, b_on, f_on):
            a, j, v = k + 1, k - 1, 1 - u
            if f_on:
                wait(dve, s["dt_ready"], NG * (j + 1))
                wait(dve, s["rd_lo"], j)
                dve.reciprocal(rd[:], dt[:]).then_inc(s["rd_ready"], 1)
            if a_on:
                wait(dve, s["x_loaded"], 16 * (a + 1))
                statistics(dve, xt, a, st, mv, s["xn_stats"], s["xn_mv"], lambda i: None, s["xn_ready"])
            if a_on:
                wait(dve, s["xn_rs"], a + 1)
                wait(dve, s["xt_psum"], KC * a)
                for i in range(SUB):
                    dve.tensor_scalar(xn[:, i, :], xt[:, i, :], mv[:, i, 0:1], rs[:, i:i + 1],
                                      ALU.subtract, ALU.mult).then_inc(s["xn_ready"], 1)
            if f_on:
                wait(dve, s["rd_hi"], j + 1)
                wait(dve, s["rb_psum"], 2 * j)
                dve.tensor_tensor(rdl[:], rd[:], rdh[:], ALU.subtract).then_inc(s["rd_lo"], 1)
            if a_on:
                for h in range(KC):
                    wait(dve, s["xt_hi"], KC * a + h + 1)
                    wait(dve, s["q_psum"], 2 * a)
                    dve.tensor_tensor(xtl[:, h, :], banks[2 + h][:], xth[:, h, :], ALU.subtract).then_inc(s["xt_lo"], 1)
            if f_on:
                for m in range(2):
                    wait(dve, s["rb_psum"], 2 * j + m + 1)
                    wait(dve, s["ou_ready"], NG * (j + 1))
                    wait(dve, s["ot_lo"], 2 * j)
                    dve.tensor_tensor(ot[:, m, :], banks[m][:], ou[:, m, :], ALU.mult).then_inc(s["ot_ready"], 1)
            if a_on:
                wait(dve, q_stacked[u], QS * (n + 1))
                for m in range(2):
                    wait(dve, s["q_hi"], 2 * a + m + 1)
                    dve.scalar_tensor_tensor(out=ql[:, m, :], in0=banks[2 + m][:], scalar=bc[:, 0, m:m + 1],
                                             in1=qh[:, m, :], op0=ALU.add, op1=ALU.subtract).then_inc(s["q_lo"], 1)
                wait(dve, s["negmax"], a)
                for i in range(SUB):
                    for g in range(NG):
                        c = NG * i + g
                        wait(dve, s["max_psum"], SUB * NG * a + c + 1)
                        dve.tensor_reduce(mx[:, i, GH * g:GH * g + GH],
                                          banks[2 + c % 2][:, 0:GROWS].rearrange("p (h s) -> p h s", h=GH),
                                          AX_X, ALU.max).then_inc(s["max_read"], 1)
                wait(dve, s["max_read"], SUB * NG * (a + 1))
                wait(dve, s["nmt_psum"], a)
                dve.tensor_scalar(nm[:], mx[:], -1.0, None, ALU.mult).then_inc(s["negmax"], 1)
            if f_on:
                dve_finish(dve, j)

        def dve_finish(dve, j):
            wait(dve, s["xr_bias"], j + 1)
            wait(dve, s["x1_stored"], 16 * j)
            wait(dve, s["x2_ready"], SUB * j)
            for m in range(2):
                wait(dve, s["wo_psum"], 2 * j + m + 1)
                for i in range(2 * m, 2 * m + 2):
                    dve.tensor_tensor(x1[:, i, :], banks[m][:, D * (i % 2):D * (i % 2) + D], xr[:, i, :],
                                      ALU.add).then_inc(s["x1_ready"], 1)
            statistics(dve, x1, j, st2, mv2, s["x2_stats"], s["x2_mv"],
                       lambda i: wait(dve, s["x1_ready"], SUB * j + i + 1), s["x2_ready"])
            wait(dve, s["x2_rs"], j + 1)
            wait(dve, s_scat, 16 * SUB * TOPK * j, 16)
            wait(dve, s["x2t_psum"], KC * j)
            for i in range(SUB):
                dve.tensor_scalar(row[:, i, 0:D], x1[:, i, :], mv2[:, i, 0:1], rs2[:, i:i + 1],
                                  ALU.subtract, ALU.mult).then_inc(s["x2_ready"], 1)
            wait(dve, s["tok_ready"], j + 1)
            dve.tensor_copy(row[:].bitcast(I32)[:, :, D], tok[:]).then_inc(s["tok_row"], 1)
            wait(dve, s["tok_row"], j + 1)
            dve.tensor_scalar(tok[:], tok[:], CH, None, ALU.add).then_inc(s["tok_ready"], 1)
            wait(dve, s["lg_psum"], j + 1)
            wait(dve, s["idx_ready"], SUB * j)
            dve.tensor_copy(lg[:], banks[0][:, 0:SUB * E].rearrange("p (i e) -> p i e", e=E)).then_inc(s["lg_ready"], 1)
            wait(dve, s["dif_ready"], j)
            wait_apart(dve, passed["dve"], s["lg_ready"], j + 1)
            for i in range(SUB):
                dve.max(top8[:, i, :], lg[:, i, :]).then_inc(s["top_ready"], 1)
            wait(dve, s["idf_ready"], j)
            for i in range(SUB):
                wait_apart(dve, passed["dve"], s["top_ready"], SUB * j + i + 1)
                dve.max_index(idx8[:, i, :], top8[:, i, :], lg[:, i, :]).then_inc(s["idx_ready"], 1)
            wait(dve, s["top_ready"], SUB * (j + 1))
            wait(dve, s["ex_ready"], j)
            dve.tensor_tensor(dif[:], top8[:, :, 1], top8[:, :, 0], ALU.subtract).then_inc(s["dif_ready"], 1)
            wait(dve, s["idx_ready"], SUB * (j + 1))
            wait(dve, s["oh_ready"], 2 * j)
            dve.tensor_copy(idf[:], idx8[:, :, 0:TOPK]).then_inc(s["idf_ready"], 1)
            wait(dve, s["idf_ready"], j + 1)
            wait(dve, s["pk_ready"], 2 * j)
            wait(dve, s["gw_ready"], 3 * j)
            wait(dve, s["both_ready"], j)
            iota = cc[:, C_IO:C_IO + 32].rearrange("p (i e) -> p i e", e=E)
            for r in range(TOPK):
                dve.tensor_tensor(oh[:, r], iota, bcast(idf[:, :, r:r + 1], [P, SUB, E]), ALU.is_equal)\
                   .then_inc(s["oh_ready"], 1)
            wait(dve, s["oh_ready"], 2 * (j + 1))
            wait(dve, s["bothb_ready"], j)
            wait(dve, s["carry_ready"], 1 + SUB * j)
            dve.tensor_tensor(both[:], oh[:, 0], oh[:, 1], ALU.add).then_inc(s["both_ready"], 1)
            wait(dve, s["both_ready"], j + 1)
            wait(dve, s["pos_psum"], j)
            dve.tensor_copy(bothb[:], both[:]).then_inc(s["bothb_ready"], 1)
            wait(dve, s["ex_ready"], j + 1)
            wait(dve, s["gate1"], j)
            dve.tensor_scalar(den[:], ex[:], 1.0, None, ALU.add).then_inc(s["den_ready"], 1)
            wait(dve, s["den_ready"], j + 1)
            wait(dve, s["gw_ready"], 3 * j)
            dve.reciprocal(gate[:, :, 0], den[:]).then_inc(s["gate0"], 1)
            wait(dve, s["gate0"], j + 1)
            dve.tensor_tensor(gate[:, :, 1], gate[:, :, 0], ex[:], ALU.mult).then_inc(s["gate1"], 1)
            dve.tensor_tensor(gw[:], oh[:, 0], bcast(gate[:, :, 0:1], [P, SUB, E]), ALU.mult).then_inc(s["gw_ready"], 1)
            wait(dve, s["gate1"], j + 1)
            dve.tensor_tensor(gw1[:], oh[:, 1], bcast(gate[:, :, 1:2], [P, SUB, E]), ALU.mult).then_inc(s["gw_ready"], 1)
            wait(dve, s["gw_ready"], 3 * j + 2)
            dve.tensor_tensor(row[:, :, D + 1:ROW], gw[:], gw1[:], ALU.add).then_inc(s["gw_ready"], 1)
            wait(dve, s["pos_psum"], j + 1)
            wait(dve, s["pos_c"], j)
            ranks = banks[1][:, 0:SUB * E].rearrange("p (i e) -> p i e", e=E)
            dve.tensor_scalar(no[:], ranks, float(CAP), BIG, ALU.is_ge, ALU.mult).then_inc(s["pos_a"], 1)
            dve.tensor_tensor(pos[:], ranks, cc[:, C_EB:C_EB + 32].rearrange("p (i e) -> p i e", e=E),
                              ALU.add).then_inc(s["pos_b"], 1)
            wait(dve, s["pos_b"], j + 1)
            wait(dve, s["pos_a"], j + 1)
            wait(dve, s["pk_ready"], 2 * j)
            dve.tensor_tensor(pos2[:], pos[:], no[:], ALU.add).then_inc(s["pos_c"], 1)
            wait(dve, s["pos_c"], j + 1)
            wait(dve, s["destf_ready"], 2 * j)
            for r in range(TOPK):
                dve.tensor_tensor(pk[:, r], oh[:, r], pos2[:], ALU.mult).then_inc(s["pk_ready"], 1)
            wait(dve, s["dest_ready"], j)
            for r in range(TOPK):
                wait(dve, s["pk_ready"], 2 * j + r + 1)
                dve.tensor_reduce(destf[:, r, :], pk[:, r], AX_X, ALU.add).then_inc(s["destf_ready"], 1)
            wait(dve, s["destf_ready"], 2 * (j + 1))
            dve.tensor_copy(dest[:], destf[:]).then_inc(s["dest_ready"], 1)
            for i in range(SUB):
                wait(dve, s["carry_ready"], 1 + SUB * j + i)
                dve.tensor_tensor(carry[:, 0, :], carry[:, 0, :], both[:, i, :], ALU.add).then_inc(s["carry_ready"], 1)
            wait(dve, s["carry_ready"], 1 + SUB * (j + 1))
            dve.tensor_copy(carryb[:], carry[:, 0, :]).then_inc(s["carryb_ready"], 1)

        @block.vector
        def _(dve):
            dve.memset(carry[:, 0, :], 0.0).then_inc(s["carry_ready"], 1)
            wait(dve, s["carry_ready"], 1)
            dve.tensor_copy(carryb[:], carry[:, 0, :]).then_inc(s["carryb_ready"], 1)
            steps(Program(dve, dve_step))

        def pool_step(pool, k, u, n, a_on, b_on, f_on):
            a, j = k + 1, k - 1
            if b_on and u == 0:
                wait(pool, s["pv_tile"], NT * k)
                for c, (dst, src, ready) in enumerate(((vsth, vraw_h, "vh_loaded"), (vstl, vraw_l, "vl_loaded"))):
                    wait(pool, s[ready], 16 * 6 * (n + 1))
                    vm = cc[0:TW, C_VM:C_VM + 192].rearrange("p (j w) -> p j w", j=3)
                    for g in range(NG):
                        mm = pool.tensor_tensor(dst[:, 3 * g:3 * g + 3, 0:64], src[:, 3 * g:3 * g + 3, :], vm, ALU.mult)
                        if g == NG - 1:
                            mm.then_inc(s["v_masked"], 1)
            if a_on:
                variance_root(pool, a, mv, ve, rs, "xn")
            for t in range(NT):
                if b_on:
                    w = TL[t % 3]
                    wait(pool, s["p_full"], NT * k + t + 1)
                    wait(pool, s["pv_tile"], NT * k + t - NP + 1)
                    pool.tensor_tensor(pl[0:w, t % NP, :], pf[0:w, t % NP, :], ph[0:w, t % NP, :],
                                       ALU.subtract).then_inc(s["p_lo"], 1)
                if f_on and t == T_OT + 1:
                    for m in range(2):
                        wait(pool, s["ot_hi"], 2 * j + m + 1)
                        wait(pool, s["wo_psum"], 2 * j)
                        pool.tensor_tensor(otl[:, m, :], ot[:, m, :], oth[:, m, :], ALU.subtract).then_inc(s["ot_lo"], 1)
                if f_on and t == T_WO - 1:
                    wait(pool, s["xr_loaded"], 16 * (j + 1))
                    pool.tensor_tensor(xr[:], xr[:], bcast(bo_row[:].rearrange("p (a d) -> p a d", a=1), [P, SUB, D]),
                                       ALU.add).then_inc(s["xr_bias"], 1)
                if f_on and t == T_WO + 1:
                    variance_root(pool, j, mv2, ve2, rs2, "x2")
            if f_on:
                wait(pool, s["dest_ready"], j + 1)
                wait(pool, s["gw_ready"], 3 * (j + 1))
                wait_apart(pool, passed["pool"], s["tok_row"], j + 1)
                for i in range(SUB):
                    for r in range(TOPK):
                        c = TOPK * i + r
                        pool.indirect_dma_start(
                            slots[:, :], bass.IndirectOffsetOnAxis(ap=dest[:].bitcast(U32)[:, r, i:i + 1], axis=0),
                            row[:, i, :], None, bounds_check=E * CAP - 1, oob_is_err=False).then_inc(s_scat, 16)

        def variance_root(pool, c, moments, plus, root, name):
            wait_apart(pool, passed["pool"], s[name + "_mv"], SUB * (c + 1))
            pool.tensor_scalar(plus[:], moments[:, :, 1], EPS, None, ALU.add).then_inc(s[name + "_ve"], 1)
            wait(pool, s[name + "_ve"], c + 1)
            wait(pool, s[name + "_ready"], SUB * c)
            pool.tensor_tensor(root[:], plus[:], half[:], ALU.pow).then_inc(s[name + "_rs"], 1)

        @block.gpsimd
        def _(pool):
            pool.iota(tok[:], pattern=[[P, SUB]], base=0, channel_multiplier=1).then_inc(s["tok_ready"], 1)
            pool.memset(half[:], -0.5).then_inc(s["half_ready"], 1)
            wait(pool, s["half_ready"], 1)
            steps(Program(pool, pool_step))
            wait(pool, s_scat, 16 * SUB * TOPK * NCH, 16)


def experts(nc, ctx, whole, passed, banks, slots, w1, b1, w2, b2, out):
    sb = lambda name, shape, dt: ctx.enter_context(nc.sbuf_tensor(name, shape, dt))
    ident = whole["cc"][:, C_ID:C_ID + P]
    w1raw, w2raw = sb("w1raw", [P, KC, HID], F32), sb("w2raw", [P, HID // P, D], F32)
    MT = HID // P
    sizes = [[min(TT, CAP - XC * c - TT * t) for t in range(3)] for c in range(NX)]
    STEPS = NX * MT
    assert all(min(z) > 64 and sum(z) % 2 == 0 for z in sizes)

    w1h = [sb(f"w1h{i}", [P, KC, HID], F32R) for i in range(2)]
    w1l = [sb(f"w1l{i}", [P, KC, HID], F32R) for i in range(2)]
    w2h = [sb(f"w2h{i}", [P, MT, D], F32R) for i in range(2)]
    w2l = [sb(f"w2l{i}", [P, MT, D], F32R) for i in range(2)]
    b1s = sb("b1s", [P, E, MT], F32)
    b2r = sb("b2r", [TT, E, D], F32)
    xin = [sb(f"xin{i}", [TT, 3, ROW], F32) for i in range(NX)]
    gcol = [sb(f"gcol{i}", [TT, 3, 1], F32) for i in range(NX)]
    xh = sb("xh", [P, 2, KC, XC], F32R)
    xl = sb("xl", [P, 2, KC, XC], F32R)
    NH = 4
    hf = sb("hf", [P, NH, XC], F32)
    hh = sb("hh", [P, NH, XC], F32R)
    hl = sb("hl", [P, NH, XC], F32R)
    b2g = sb("b2g", [TT, 2, 3, D], F32)
    ys = sb("ys", [TT, 2, 3, D], F32)
    XT, HB, YB = banks[0:2], [banks[2], banks[3], banks[7]], banks[4:7]

    s, x_in, added, s_w = whole["e"], whole["x_in"], whole["added"], whole["s_w"]
    block = ctx.enter_context(nc.Block())

    def pairs(eng, turn):
        with eng.Fori(0, E // 2 - 1) as b:
            turn(eng, b, False)
        turn(eng, E // 2 - 1, True)

    def chunks(b, last):
        for eo in range(2):
            for c in range(NX):
                e = 2 * b + eo
                yield e, eo, c, NX * e + c, not (last and eo == 1 and c == NX - 1)

    def sync_pair(sp, b, last):
        for e, eo, c, q, _ in chunks(b, last):
            wait(sp, added[c], 48 * e, 16)
            lo, two, z = e * CAP + XC * c, 2 * TT, sizes[c][2]
            front = slots[bass.ds(lo, two), :].rearrange("(t p) r -> p t r", p=TT)
            sp.dma_start(xin[c][:, 0:2, :], front).then_inc(x_in[c], 16)
            sp.dma_start(xin[c][0:z, 2, :], slots[bass.ds(lo + two, z), :]).then_inc(x_in[c], 16)
            sp.dma_start(gcol[c][:, 0:2, :], slots[bass.ds(lo, two), bass.ds(D + 1 + e, 1)]
                         .rearrange("(t p) r -> p t r", p=TT), allow_slow_non_contiguous=True).then_inc(x_in[c], 16)
            sp.dma_start(gcol[c][0:z, 2, :], slots[bass.ds(lo + two, z), bass.ds(D + 1 + e, 1)],
                         allow_slow_non_contiguous=True).then_inc(x_in[c], 16)
            if c == 0 and not (last and eo == 1):
                wait(sp, s["w_split"], 2 * (e + 1))
                sp.dma_start(w1raw[:], w1[e + 1]).then_inc(s_w, 16)
                sp.dma_start(w2raw[:], w2[e + 1]).then_inc(s_w, 16)

    @block.sync
    def _(sp):
        sp.dma_start(b1s[:], b1).then_inc(s["b1_loaded"], 16)
        sp.dma_start(w1raw[:], w1[0]).then_inc(s_w, 16)
        sp.dma_start(w2raw[:], w2[0]).then_inc(s_w, 16)
        pairs(sp, sync_pair)

    def transpose_x(pe, e, c, q):
        wait(pe, x_in[c], 64 * (e + 1))
        for kc in range(KC):
            for t, z in enumerate(sizes[c]):
                mm = pe.transpose(XT[kc][:, TT * t:TT * t + z], xin[c][0:z, t, P * kc:P * kc + P], ident[0:z, 0:z])
            mm.then_inc(s["xt_psum"], 1)

    def layer1(pe, e, eo, c, q, m):
        n, at, g = sum(sizes[c]), MT * c + m, STEPS * e + MT * c + m
        o = HB[at % 3][:, 0:n]
        if m == 0:
            wait(pe, s["xt_low"], KC * (q + 1))
            if c == 0:
                wait(pe, s["w_split"], 2 * e + 1)
        if eo or at >= 3:
            wait(pe, s["h_full"], g - 2)
        x0 = (NX * eo + c) % 2
        k = 0
        for w_, x_ in ((w1h, xh), (w1h, xl), (w1l, xh)):
            for kc in range(KC):
                mm = pe.matmul(o, w_[eo][:, kc, P * m:P * m + P], x_[:, x0, kc, 0:n], start=(k == 0), stop=(k == 5))
                k += 1
        mm.then_inc(s["h_psum"], 1)

    def layer2(pe, e, eo, c, q, m):
        g = STEPS * e + MT * c + m
        if m == 0:
            wait(pe, s["y_ready"], 3 * q)
            if c == 0:
                wait(pe, s["w_split"], 2 * e + 2)
        wait(pe, s["h_low"], g + 1)
        for t, z in enumerate(sizes[c]):
            for h_, w_ in ((hh, w2h), (hh, w2l), (hl, w2h)):
                first, final = m == 0 and h_ is hh and w_ is w2h, m == MT - 1 and h_ is hl
                mm = pe.matmul(YB[t][0:z, 0:D], h_[:, m % NH, TT * t:TT * t + z], w_[eo][:, m, :],
                               start=first, stop=final)
        mm.then_inc(s["l2_done"], 1)

    def pe_pair(pe, b, last):
        behind = []
        for e, eo, c, q, follows in chunks(b, last):
            for m in range(MT):
                layer1(pe, e, eo, c, q, m)
                behind.append((e, eo, c, q, m))
                if len(behind) > 2:
                    layer2(pe, *behind.pop(0))
                if m == 4 and follows:
                    transpose_x(pe, e + (c == NX - 1), (c + 1) % NX, q + 1)
        for one in behind:
            layer2(pe, *one)

    @block.tensor
    def _(pe):
        transpose_x(pe, 0, 0, 0)
        pairs(pe, pe_pair)

    def round_x(act, c, q, x0):
        n = sum(sizes[c])
        wait(act, s["h_psum"], MT * (q - 1))
        for kc in range(KC):
            wait(act, s["xt_psum"], KC * q + kc + 1)
            act.activation(xh[:, x0, kc, 0:n], XT[kc][:, 0:n], ACT.Copy).then_inc(s["xt_high"], 1)

    def act_pair(act, b, last):
        for e, eo, c, q, follows in chunks(b, last):
            n = sum(sizes[c])
            for m in range(MT):
                at, g = MT * c + m, STEPS * e + MT * c + m
                wait(act, s["l2_done"], STEPS * e if not eo and at < NH else g - NH + 1)
                wait_apart(act, passed["act"], s["h_psum"], g + 1)
                for h_, ready in ((hh, "h_high"), (hf, "h_full")):
                    act.activation(h_[:, m % NH, 0:n], HB[at % 3][:, 0:n], ACT.Gelu_apprx_tanh,
                                   bias=b1s[:, e, m:m + 1]).then_inc(s[ready], 1)
                if m == 4 and follows:
                    round_x(act, (c + 1) % NX, q + 1, (NX * eo + c + 1) % 2)

    @block.scalar
    def _(act):
        wait(act, s["b1_loaded"], 16)
        round_x(act, 0, 0, 0)
        pairs(act, act_pair)

    def split_weights(dve, e, eo, part):
        raw, high, low = ((w1raw, w1h, w1l), (w2raw, w2h, w2l))[part // 2]
        if part % 2 == 0:
            wait(dve, s_w, 32 * (e + 1))
            wait(dve, s["l2_done"], STEPS * (e - 1))
            dve.tensor_copy(high[eo][:], raw[:]).then_inc(s["w_high"], 1)
        else:
            wait(dve, s["w_high"], 2 * e + part // 2 + 1)
            dve.tensor_tensor(low[eo][:], raw[:], high[eo][:], ALU.subtract).then_inc(s["w_split"], 1)

    def rest_x(dve, c, q, x0):
        n = sum(sizes[c])
        for kc in range(KC):
            wait(dve, s["xt_high"], KC * q + kc + 1)
            dve.tensor_tensor(xl[:, x0, kc, 0:n], XT[kc][:, 0:n], xh[:, x0, kc, 0:n], ALU.subtract)\
               .then_inc(s["xt_low"], 1)

    def outputs(dve, e, eo, c, q):
        y0 = (NX * eo + c) % 2
        wait(dve, s["l2_done"], MT * (q + 1))
        wait(dve, s["b2g_ready"], 3 * (q + 1))
        if c >= 2:
            wait(dve, added[c - 2], 48 * (e + 1), 16)
        else:
            wait(dve, added[c + 1], 48 * e, 16)
        for t, z in enumerate(sizes[c]):
            dve.scalar_tensor_tensor(out=ys[0:z, y0, t, :], in0=YB[t][0:z, 0:D], scalar=gcol[c][0:z, t, :],
                                     in1=b2g[0:z, y0, t, :], op0=ALU.mult, op1=ALU.add).then_inc(s["y_ready"], 1)

    def dve_pair(dve, b, last):
        behind = None
        for e, eo, c, q, follows in chunks(b, last):
            n = sum(sizes[c])
            for m in range(MT):
                g = STEPS * e + MT * c + m
                wait(dve, s["h_full"], g + 1)
                dve.tensor_tensor(hl[:, m % NH, 0:n], hf[:, m % NH, 0:n], hh[:, m % NH, 0:n], ALU.subtract)\
                   .then_inc(s["h_low"], 1)
                if m == 2 and behind:
                    outputs(dve, *behind)
                if c == 1 and m % 2 and not (last and eo == 1):
                    split_weights(dve, e + 1, 1 - eo, m // 2)
                if m == 4 and follows:
                    rest_x(dve, (c + 1) % NX, q + 1, (NX * eo + c + 1) % 2)
            behind = (e, eo, c, q)
        outputs(dve, *behind)

    @block.vector
    def _(dve):
        for part in range(4):
            split_weights(dve, 0, 0, part)
        rest_x(dve, 0, 0, 0)
        pairs(dve, dve_pair)

    def pool_pair(pool, b, last):
        for e, eo, c, q, _ in chunks(b, last):
            y0 = (NX * eo + c) % 2
            wait(pool, s["y_ready"], 3 * q)
            wait_apart(pool, passed["pool"], x_in[c], 64 * (e + 1))
            for t, z in enumerate(sizes[c]):
                pool.tensor_tensor(b2g[0:z, y0, t, :], b2r[0:z, e, :], gcol[c][0:z, t, :].to_broadcast([z, D]),
                                   ALU.mult).then_inc(s["b2g_ready"], 1)
            for t, z in enumerate(sizes[c]):
                if t:
                    wait(pool, added[c], 48 * e + 16 * t, 16)
                elif c:
                    wait(pool, added[c - 1], 48 * (e + 1), 16)
                else:
                    wait(pool, added[NX - 1], 48 * e, 16)
                wait_apart(pool, passed["pool"], s["y_ready"], 3 * q + t + 1)
                pool.indirect_dma_start(
                    out[:, :], bass.IndirectOffsetOnAxis(ap=xin[c][0:z, t, D:D + 1].bitcast(U32), axis=0),
                    ys[0:z, y0, t, :], None, bounds_check=NTOK - 1, oob_is_err=False,
                    compute_op=ALU.add).then_inc(added[c], 16)

    @block.gpsimd
    def _(pool):
        part = TT // NX
        for c in range(NX):
            pool.dma_start(b2r[part * c:part * c + part], b2[:, :].rearrange("(a e) d -> a e d", a=1)
                           .to_broadcast([part, E, D])).then_inc(added[c], 16)
        for c in range(NX):
            pool.wait_ge(added[c], 16)
        pairs(pool, pool_pair)
        for c in range(NX):
            wait(pool, added[c], 48 * E, 16)


def kernel(**inputs):
    import numpy as np
    import concourse.bacc as bacc
    from concourse.bass_utils import run_bass_kernel_spmd

    a = {k: np.asarray(v) for k, v in inputs.items()}
    g = lambda name: a["L0_" + name]
    rows = lambda w: w.reshape(-1, P, w.shape[-1]).transpose(1, 0, 2)
    columns = lambda v: v.reshape(-1, P).T
    arrays = {
        "x": a["x"].reshape(NTOK, D),
        "ctxT": rows(a["ctx_1024"].reshape(B * S, D).T),
        "watt": np.stack([rows(g("xattn_W" + n)) for n in "kvqo"], axis=1),
        "wg": rows(g("ffn_Wg")),
        "bcols": np.stack([columns(g("xattn_b" + n)) for n in "qk"], axis=1),
        "brows": np.stack([g("xattn_bv"), g("xattn_bo")]),
        "w1": g("ffn_W1").reshape(E, KC, P, HID).transpose(0, 2, 1, 3),
        "b1": g("ffn_b1").reshape(E, HID // P, P).transpose(2, 0, 1),
        "w2": g("ffn_W2").reshape(E, HID // P, P, D).transpose(0, 2, 1, 3),
        "b2": g("ffn_b2"),
        "cst": constants(np),
    }
    arrays = {k: np.ascontiguousarray(v) for k, v in arrays.items()}
    nc = bacc.Bacc("TRN2", target_bir_lowering=False, num_devices=1)
    aps = {k: nc.dram_tensor(k, v.shape, F32, kind="ExternalInput").ap() for k, v in arrays.items()}
    out = nc.dram_tensor("out", (NTOK, D), F32, kind="ExternalOutput").ap()
    build(nc, out=out, **aps)
    r = run_bass_kernel_spmd(nc, [arrays], core_ids=[0])
    return r.results[0]["out"].reshape(B, L, D)
```

```python
from contextlib import ExitStack

import concourse.bass as bass
from concourse import mybir
from concourse.alu_op_type import AluOpType as ALU

F32 = mybir.dt.float32
F32R = mybir.dt.float32r
BF16 = mybir.dt.bfloat16
I32 = mybir.dt.int32
U32 = mybir.dt.uint32
ACT = mybir.ActivationFunctionType
AX_X = mybir.AxisListType.X

P = 128
B, L, D = 4, 1024, 256
S, H = 77, 16
HD = D // H
SCALE = HD ** -0.5
EPS = 1e-5
E, HID, TOPK = 8, 1024, 2
NTOK = B * L
CAP = -(-NTOK * TOPK * 105 // (E * 100))
CH = 512
NCH = NTOK // CH
SUB = CH // P
KC = D // P
GH = 4
NG = H // GH
GROWS = GH * S
TL = [104, 102, 102]
TO = [0, 104, 206]
TW = max(TL)
NT = NG * len(TL)
TT = 120
XC = 3 * TT
NX = -(-CAP // XC)
ROW = D + 1 + E
BIG = 100000.0
KROWS = 3 * 2 * HD + H


T_XT, T_Q, T_MAX, T_NEGMAX = 0, 1, (2, 4, 5, 6), 7
T_SPREAD, T_WO, T_X2T, T_LOGITS, T_EX, T_POS = 2, 3, 8, 9, 10, 11


def segments():
    out = []
    for hl in range(GH):
        for j in range(len(TL)):
            lo, hi = max(hl * S, TO[j]), min((hl + 1) * S, TO[j] + TL[j])
            if lo < hi:
                out.append((hl, j, lo - TO[j], lo - hl * S, hi - lo))
    return out


C_ID = 0
C_TRI = C_ID + P
C_SEL = C_TRI + P
C_BLK = C_SEL + 2 * P
C_ON = C_BLK + 8 * S
C_OH = C_ON + 3 * P
C_IO = C_OH + NT * TW
C_EB = C_IO + TOPK * SUB * E
C_START = C_EB + SUB * E
C_N = C_START + E


def constants(np):
    c = np.zeros((P, C_N), np.float32)
    c[:, C_ID:C_ID + P] = np.eye(P)
    c[:, C_TRI:C_TRI + P] = np.triu(np.ones((P, P)), 1)
    for g in range(NG):
        for hl in range(GH):
            at = C_SEL + (g // 2) * P + 64 * (g % 2) + HD * hl
            c[32 * g + 8 * hl, at:at + HD] = 1
    for h in range(8):
        c[HD * h:HD * h + HD, C_BLK + S * h:C_BLK + S * h + S] = 1
    for hl, j, p0, _, n in segments():
        c[p0:p0 + n, C_ON + P * j + 64 + 8 * hl:C_ON + P * j + 64 + 8 * hl + 8] = 1
        for g in range(NG):
            t = 3 * g + j
            c[96 + GH * g + hl, C_OH + TW * t + p0:C_OH + TW * t + p0 + n] = 1
    c[:, C_IO:C_IO + TOPK * SUB * E] = np.tile(np.arange(E), TOPK * SUB)
    c[:, C_EB:C_EB + SUB * E] = np.tile(np.arange(E) * CAP + CAP, SUB)
    for e in range(E):
        c[:, C_START + e] = [(e * CAP * (p + 1)) // P - (e * CAP * p) // P for p in range(P)]
    return c


COUNTS = """xn_stats xn_mv xn_ve xn_rs xn_ready xt_psum xt_ready q_psum q_hi q_lo max_psum max_read negmax
    nmt_psum nmt_ready sc_psum p_ready pv_tile ou_ready dt_ready rd_ready rb_psum ot_ready wo_psum
    xr_bias x1_ready x1_stored x2_stats x2_mv x2_ve x2_rs x2_ready tok_ready x2t_psum x2t_ready lg_psum
    top_ready idx_ready idf_ready dif_ready ex_ready den_ready gate0 gate1 oh_ready gw_ready gate_row
    bothb_ready chosen carry_ready carryb_ready pos_psum over place pk_ready destf_ready dest_ready
    tok_row x_loaded xr_loaded kbm_loaded k_loaded0 k_loaded1 v_loaded0 v_loaded1 pool_set""".split()
EXPERT_COUNTS = """w_high w_split b1_loaded xt_psum xt_high xt_low h_psum h_high h_full h_low l2_done
    y_psum b2g_ready y_ready""".split()


def prime(eng, semaphores):
    for one in semaphores:
        eng.sem_inc(one, 1)


def after(count, primed=1):
    return (max(count, 0) if isinstance(count, int) else count) + primed


def build(nc, x, ctxT, watt, wg, bcols, brows, w1, b1, w2, b2, cst, out):
    slots = nc.dram_tensor("slots", (E * CAP, ROW), F32, kind="Internal").ap()
    with ExitStack() as top:
        sb = lambda name, shape, dt: top.enter_context(nc.sbuf_tensor(name, shape, dt))
        sem = lambda name: top.enter_context(nc.semaphore(name))
        whole = dict(
            cc=sb("cc", [P, C_N], F32), row=sb("row", [P, 2, SUB, ROW], F32), dest=sb("dest", [P, 2, TOPK, SUB], I32),
            w1raw=sb("w1raw", [P, KC, HID], F32), w2raw=sb("w2raw", [P, HID // P, D], F32), s_init=sem("s_init"), s_scat=[sem(f"s_scat{u}") for u in range(2)],
            s={n: sem("s_" + n) for n in COUNTS}, q_stacked=[sem(f"s_q_stacked{u}") for u in range(2)],
            e={n: sem("e_" + n) for n in EXPERT_COUNTS}, s_w=sem("e_weights"),
            x_in=[sem(f"e_x_in{i}") for i in range(NX)], added=[sem(f"e_added{i}") for i in range(NX)])
        passed = {n: sem("passed_" + n) for n in ("act", "dve", "pool")}
        banks = [top.enter_context(nc.psum_tensor(f"bank{i}", [P, 512], F32)) for i in range(8)]
        with ExitStack() as att:
            attention_and_routing(nc, att, whole, passed, banks, slots, x, ctxT, watt, wg, bcols, brows, w1, w2, cst, out)
        with ExitStack() as ffn:
            experts(nc, ffn, whole, passed, banks, slots, w1, b1, w2, b2, out)


def attention_and_routing(nc, ctx, whole, passed, banks, slots, x, ctxT, watt, wg, bcols, brows, w1, w2, cst, out):
    sb = lambda name, shape, dt: ctx.enter_context(nc.sbuf_tensor(name, shape, dt))
    sem = lambda name: ctx.enter_context(nc.semaphore(name))
    cc, s_init, s_scat = whole["cc"], whole["s_init"], whole["s_scat"]
    s, q_stacked = whole["s"], whole["q_stacked"]
    ident = cc[:, C_ID:C_ID + P]

    wq = sb("wq", [P, KC, D], F32)
    wo = sb("wo", [P, KC, D], F32)
    wgs = sb("wgs", [P, KC, E], F32)
    bc = sb("bc", [P, 2, KC], F32)
    bo_row = sb("bo_row", [P, D], F32)
    tri = sb("tri", [P, P], BF16)
    ones = sb("ones", [P, P], BF16)
    kst = sb("kst", [KROWS, NT, TW], F32R)
    vst = sb("vst", [TW, NT, P], F32)
    vf = sb("vf", [S, B, D], F32)
    fill = sb("fill", [P, ROW], F32)
    k_tiles = nc.dram_tensor("k_tiles", (B, P, NT, TW), F32, kind="Internal").ap()
    s_diag, s_kept, s_kept_low = sem("s_diag"), sem("s_kept"), sem("s_kept_low")
    k_diag = nc.dram_tensor("k_diag", (B, P, 2 * 8 * S), F32, kind="Internal").ap()

    kbm = sb("kbm", [P, 2, 8 * S], F32R)
    xt = sb("xt", [P, SUB, D], F32)
    st = sb("st", [P, SUB, 6], F32)
    mv = sb("mv", [P, SUB, 2], F32)
    ve = sb("ve", [P, SUB], F32)
    rs = sb("rs", [P, SUB], F32)
    half = sb("half", [P, SUB], F32)
    xn = sb("xn", [P, SUB, D], F32)
    xT = sb("xT", [P, KC, CH], F32)
    qh = sb("qh", [P, 2, CH], F32R)
    ql = sb("ql", [P, 2, CH], F32R)
    mx = sb("mx", [P, SUB, H], F32)
    nm = sb("nm", [P, SUB, H], F32)
    nmt = sb("nmt", [H, CH], F32R)
    qs = sb("qs", [KROWS, 2, NT, CH], F32R)
    st2 = sb("st2", [P, SUB, 6], F32)
    mv2 = sb("mv2", [P, SUB, 2], F32)
    ve2 = sb("ve2", [P, SUB], F32)
    rs2 = sb("rs2", [P, SUB], F32)
    row, dest = whole["row"], whole["dest"]
    top8 = sb("top8", [P, SUB, 8], F32)
    idx8 = sb("idx8", [P, SUB, 8], U32)
    idf = sb("idf", [P, TOPK, SUB], F32)
    dif = sb("dif", [P, SUB], F32)
    ex = sb("ex", [P, SUB], F32)
    den = sb("den", [P, SUB], F32)
    gate = sb("gate", [P, TOPK, SUB], F32)
    oh = sb("oh", [P, TOPK, SUB, E], F32)
    gw = sb("gw", [P, TOPK, SUB, E], F32)
    bothb = sb("bothb", [P, SUB, E], BF16)
    chosen = sb("chosen", [P, E], F32)
    carry = sb("carry", [P, E], F32)
    carryb = sb("carryb", [P, E], BF16)
    over = sb("over", [P, SUB, E], F32)
    place = sb("place", [P, SUB, E], F32)
    pk = sb("pk", [P, TOPK, SUB, E], F32)
    destf = sb("destf", [P, TOPK * SUB], F32)
    tok = sb("tok", [P, SUB], I32)

    with ExitStack() as pre:
        psb = lambda name, shape, dt: pre.enter_context(nc.sbuf_tensor(name, shape, dt))
        psem = lambda name: pre.enter_context(nc.semaphore(name))
        wkv = psb("wkv", [P, 2, KC, D], F32)
        cx = psb("cx", [P, KC, B * S], F32)
        bv_row = psb("bv_row", [P, D], F32)
        kf = psb("kf", [P, 2, B * S], F32)
        kh = psb("kh", [P, 2, B * S], F32R)
        kl = psb("kl", [P, 2, B * S], F32R)
        kbh = psb("kbh", [P, B, 2, 8 * S], F32R)
        kbl = psb("kbl", [P, B, 2, 8 * S], F32R)
        hot = psb("hot", [KROWS, NT, TW], F32R)
        s_ctx, s_wk, s_rest, s_cst, s_pre, s_k, s_v, s_kf, s_kh, s_kl, s_vf, s_fill, s_kbh, s_kbl, s_hot = (
            psem("p_" + n) for n in
            "ctx wk rest cst pre k v kf kh kl vf fill kbh kbl hot".split())
        block = pre.enter_context(nc.Block())
        blk = cc[:, C_BLK:C_BLK + 616].rearrange("p (h s) -> p h s", h=8)

        def diagonal(eng, dst, src, b, m, ready):
            eng.tensor_tensor(dst[:, b, m, :].rearrange("p (h s) -> p h s", h=8),
                              src[:, m, b * S:b * S + S].rearrange("p (a s) -> p a s", a=1).to_broadcast([P, 8, S]),
                              blk, ALU.mult).then_inc(ready, 1)

        @block.sync
        def _(sp):
            sp.dma_start(cx[:], ctxT).then_inc(s_ctx, 16)
            sp.dma_start(cc[:], cst).then_inc(s_cst, 16)
            sp.dma_start(wq[:], watt[:, 2]).then_inc(s_rest, 16)
            sp.dma_start(wo[:], watt[:, 3]).then_inc(s_rest, 16)
            sp.dma_start(wgs[:], wg).then_inc(s_rest, 16)
            sp.dma_start(bo_row[:], brows[1:2, :].to_broadcast([P, D])).then_inc(s_rest, 16)
            for group in (s.values(), q_stacked, whole["e"].values(), [whole["s_w"]], whole["x_in"]):
                prime(sp, group)
            sp.wait_ge(s_rest, 64)

        @block.scalar
        def _(act):
            act.dma_start(wkv[:], watt[:, 0:2]).then_inc(s_wk, 16)
            act.dma_start(bc[:], bcols).then_inc(s_wk, 16)
            act.dma_start(bv_row[:], brows[0:1, :].to_broadcast([P, D])).then_inc(s_wk, 16)
            act.wait_ge(s_cst, 16)
            act.activation(hot[96:112, :, :], cc[96:112, C_OH:C_OH + NT * TW].rearrange("p (t w) -> p t w", t=NT),
                           ACT.Copy).then_inc(s_hot, 1)
            act.activation(tri[:], cc[:, C_TRI:C_TRI + P], ACT.Copy).then_inc(s_pre, 1)
            for g in range(NG):
                act.activation(vst[:, 3 * g:3 * g + 3, :],
                               cc[0:TW, C_ON:C_ON + 3 * P].rearrange("p (j w) -> p j w", j=3), ACT.Copy).then_inc(s_pre, 1)
            act.wait_ge(s_hot, 1)
            for b in range(B):
                act.dma_start(k_tiles[b, 96:112], hot[96:112].bitcast(F32)).then_inc(s_kept, 16)

        @block.tensor
        def _(pe):
            pe.wait_ge(s_ctx, 16)
            pe.wait_ge(s_wk, 48)
            for m in range(2):
                for kc in range(KC):
                    mm = pe.matmul(banks[m][:, 0:B * S], wkv[:, 0, kc, P * m:P * m + P], cx[:, kc, :],
                                   start=(kc == 0), stop=(kc == KC - 1))
                mm.then_inc(s_k, 1)
            for b in range(B):
                for kc in range(KC):
                    mm = pe.matmul(banks[2 + b][0:S, 0:D], cx[:, kc, b * S:b * S + S], wkv[:, 1, kc, :],
                                   start=(kc == 0), stop=(kc == KC - 1))
                mm.then_inc(s_v, 1)

        @block.vector
        def _(dve):
            dve.memset(ones[:], 1.0).then_inc(s_pre, 1)
            for m in range(2):
                dve.wait_ge(s_k, m + 1)
                dve.tensor_scalar(kf[:, m, :], banks[m][:, 0:B * S], bc[:, 1, m:m + 1], None, ALU.add).then_inc(s_kf, 1)
                dve.wait_ge(s_kf, m + 1)
                dve.tensor_copy(kh[:, m, :], kf[:, m, :]).then_inc(s_kh, 1)
                dve.wait_ge(s_kh, m + 1)
                dve.tensor_tensor(kl[:, m, :], kf[:, m, :], kh[:, m, :], ALU.subtract).then_inc(s_kl, 1)
            dve.wait_ge(s_cst, 16)
            for b in range(B):
                for m in range(2):
                    diagonal(dve, kbh, kh, b, m, s_kbh)
            dve.wait_ge(s_kl, 2)
            for b in range(2, B):
                for m in range(2):
                    diagonal(dve, kbl, kl, b, m, s_kbl)
            for b in range(B):
                dve.wait_ge(s_v, b + 1)
                dve.tensor_tensor(vf[:, b, :], banks[2 + b][0:S, 0:D], bv_row[0:S, :], ALU.add).then_inc(s_vf, 1)

        @block.gpsimd
        def _(pool):
            pool.memset(fill[:], 0.0).then_inc(s_fill, 1)
            pool.wait_ge(s_fill, 1)
            pool.memset(fill[:].bitcast(I32)[:, D:D + 1], int(BIG)).then_inc(s_fill, 1)
            pool.wait_ge(s_fill, 2)
            done = E * CAP // P * P
            for i, (lo, hi) in enumerate(((done, done + 1), (done + 1, E * CAP))):
                pool.dma_start(slots[lo:hi, :], fill[0:hi - lo, :]).then_inc(s_scat[i], 16)
            pool.wait_ge(s_cst, 16)
            pool.wait_ge(s_kl, 2)
            for b in range(2):
                for m in range(2):
                    diagonal(pool, kbl, kl, b, m, s_kbl)
            for one in s_scat:
                pool.wait_ge(one, 16)

    xr = sb("xr", [P, SUB, D], F32)
    NP = 4
    pr = sb("pr", [TW, NP, CH], F32)
    ou = sb("ou", [P, 2, CH], F32)
    dt = sb("dt", [P, CH], F32)
    rd = sb("rd", [P, CH], F32)
    ot = sb("ot", [P, 2, CH], F32)
    x1 = sb("x1", [P, SUB, D], F32)
    x2t = sb("x2t", [P, KC, CH], F32)

    QS = 16 * 19
    xv = x.rearrange("(c i p) d -> c p i d", i=SUB, p=P)
    ov = out.rearrange("(c i p) d -> c p i d", i=SUB, p=P)
    SC, PV = banks[4:6], banks[6:8]
    SLOT_ROWS = E * CAP // P
    FILLS = 6
    assert SLOT_ROWS * P * TOPK >= 0

    def steps(eng, step):
        for k in (-2, -1, 0):
            step(eng, k, k % 2, k // 2, True, k >= -1, k >= 0, False)
        with eng.Fori(0, NCH // 2 - 2) as b:
            step(eng, 2 * b + 1, 1, b, True, True, True, True)
            step(eng, 2 * b + 2, 0, b + 1, True, True, True, True)
        for k in range(NCH - 3, NCH + 1):
            step(eng, k, k % 2, k // 2, k < NCH - 2, k < NCH - 1, k < NCH, True)

    def bcast(ap, shape):
        return ap.to_broadcast(shape)

    with ExitStack() as main:
        block = main.enter_context(nc.Block())

        def sync_step(sp, k, u, n, ln_on, a_on, b_on, f_on):
            a, j, v = k + 1, k - 1, 1 - u
            if f_on:
                sp.wait_ge(s["x1_ready"], after(SUB * j))
                sp.dma_start(xr[:], xv[j]).then_inc(s["xr_loaded"], 16)
            if ln_on:
                sp.wait_ge(s["xn_ready"], after(SUB * (a + 1)))
                sp.dma_start(xt[:], xv[a + 1]).then_inc(s["x_loaded"], 16)
            if not a_on and not f_on:
                for b0, b1 in ((0, 1), (1, B)):
                    sp.dma_start(k_diag[b0:b1].rearrange("b p c -> p b c"),
                                 kbh[:, b0:b1].bitcast(F32).rearrange("p b m c -> p b (m c)")).then_inc(s_diag, 16)
                    if b0 == 0:
                        keep_keys(sp, 0, kbh, s_kept)
            if a_on and u == 1:
                sp.wait_ge(s_diag, 32)
                sp.wait_ge(s["max_psum"], after(SUB * NG * a))
                sp.dma_start(kbm[:].bitcast(F32).rearrange("p m c -> p (m c)"), k_diag[n + 1])\
                  .then_inc(s["kbm_loaded"], 16)
            if b_on and u == 0:
                stationary(sp, k, n, 1)
            if a_on:
                sp.wait_ge(s["q_lo"], after(2 * (a + 1)))
                sp.wait_ge(s["sc_psum"], after(NT * k))
                for m in range(2):
                    for t in range(3):
                        p0 = 64 * m + HD * t
                        for r, src in ((0, qh), (32, qh), (64, ql)):
                            sp.dma_start(qs[r:r + 32, v, 3 * m + t:NT:6, :].bitcast(F32),
                                         src[p0:p0 + 32, :, :].bitcast(F32)).then_inc(q_stacked[v], 16)
            if f_on:
                sp.wait_ge(s["x1_ready"], after(SUB * (j + 1)))
                sp.dma_start(ov[j], x1[:]).then_inc(s["x1_stored"], 16)
            if a_on:
                sp.wait_ge(s["nmt_ready"], after(a + 1))
                sp.dma_start(qs[96:112, v, :, :].bitcast(F32),
                             bcast(nmt[:].bitcast(F32).rearrange("h (a c) -> h a c", a=1), [H, NT, CH])).then_inc(q_stacked[v], 16)
            if a_on and u == 1:
                stationary(sp, a, n + 1, 0)
            if a_on and not f_on:
                for part in range(FILLS * (k + 1) // 2, FILLS * (k + 2) // 2):
                    lo, hi = SLOT_ROWS * part // FILLS, SLOT_ROWS * (part + 1) // FILLS
                    sp.dma_start(slots[lo * P:hi * P, :].rearrange("(n p) r -> p n r", p=P),
                                 bcast(fill[:].rearrange("p (a r) -> p a r", a=1), [P, hi - lo, ROW])).then_inc(s_init, 16)

        def keep_keys(eng, r, part, kept):
            for m in range(2):
                for t in range(3):
                    p0, lo = 64 * m + HD * t, GROWS * m + TO[t]
                    for half in range(2):
                        eng.dma_start(k_tiles[:, r:r + 32, 3 * m + t + 6 * half, 0:TL[t]].rearrange("b r c -> r b c"),
                                      part[p0:p0 + 32, :, half, lo:lo + TL[t]].bitcast(F32)).then_inc(kept, 16)

        def stationary(sp, c, n, half):
            t0, g0 = 6 * half, 2 * half
            sp.wait_ge(s_kept, 16 * (24 + B))
            sp.wait_ge(s_kept_low, 16 * 12)
            sp.wait_ge(s["sc_psum"], after(NT * (c - 1) + t0 + 6))
            for t in range(3):
                sp.dma_start(kst[:, t0 + t:t0 + 6:3, 0:TL[t]].bitcast(F32),
                             k_tiles[n, 0:KROWS, t0 + t:t0 + 6:3, 0:TL[t]]).then_inc(s[f"k_loaded{half}"], 16)
            sp.wait_ge(s["pv_tile"], after(NT * (c - 1) + t0 + 6))
            for hl, t, p0, s0, rows in segments():
                src = vf[s0:s0 + rows, bass.ds(n, 1), 64 * g0:64 * g0 + 128].rearrange("p a (g w) -> p (a g) w", g=2)
                sp.dma_start(vst[p0:p0 + rows, t0 + t:t0 + 6:3, HD * hl:HD * hl + HD],
                             src[:, :, HD * hl:HD * hl + HD]).then_inc(s[f"v_loaded{half}"], 16)

        @block.sync
        def _(sp):
            steps(sp, sync_step)
            sp.dma_start(whole["w1raw"][:], w1[0]).then_inc(whole["s_w"], 16)
            sp.dma_start(whole["w2raw"][:], w2[0]).then_inc(whole["s_w"], 16)
            sp.wait_ge(s["x1_stored"], after(16 * NCH))

        def pe_scores(pe, k, u, n, t):
            if t == 0:
                pe.wait_ge(q_stacked[u], after(QS * (n + 1)))
            if t in (0, 6):
                pe.wait_ge(s[f"k_loaded{t // 6}"], after(16 * 3 * (n + 1)))
            pe.wait_ge(s["p_ready"], after(NT * k + t - 1))
            pe.matmul(SC[t % 2][0:TL[t % 3], :], kst[:, t, 0:TL[t % 3]], qs[:, u, t, :],
                      start=True, stop=True).then_inc(s["sc_psum"], 1)

        def pe_values(pe, k, n, t):
            g, w = t // 3, TL[t % 3]
            if t % 3 == 0:
                pe.wait_ge(s["dt_ready"], after(NG * k + g - 1))
            if t in (0, 6):
                pe.wait_ge(s[f"v_loaded{t // 6}"], after(16 * 6 * (n + 1)))
            pe.wait_ge(s["p_ready"], after(NT * k + t + 1))
            pe.matmul(PV[g % 2][:], vst[0:w, t, :], pr[0:w, t % NP, :], start=(t % 3 == 0), stop=(t % 3 == 2))\
              .then_inc(s["pv_tile"], 1)

        def pe_step(pe, k, u, n, ln_on, a_on, b_on, f_on):
            a, j, v = k + 1, k - 1, 1 - u
            ba = n + 1 if u == 1 else n
            for t in range(NT):
                if b_on:
                    pe_scores(pe, k, u, n, t)
                    if t >= 2:
                        pe_values(pe, k, n, t - 2)
                if a_on and t == T_XT:
                    pe.wait_ge(s["nmt_ready"], after(a))
                    for h in range(KC):
                        for i in range(SUB):
                            pe.wait_ge(s["xn_ready"], after(SUB * a + i + 1))
                            mm = pe.transpose(banks[2 + h][:, P * i:P * i + P], xn[:, i, P * h:P * h + P], ident)
                        mm.then_inc(s["xt_psum"], 1)
                if a_on and t == T_Q:
                    pe.wait_ge(s["xt_ready"], after(KC * (a + 1)))
                    for m in range(2):
                        for kc in range(KC):
                            mm = pe.matmul(banks[2 + m][:], wq[:, kc, P * m:P * m + P], xT[:, kc, :],
                                           start=(kc == 0), stop=(kc == KC - 1))
                        mm.then_inc(s["q_psum"], 1)
                if f_on and t == T_SPREAD:
                    pe.wait_ge(s["rd_ready"], after(j + 1))
                    pe.wait_ge(s["over"], after(j))
                    pe.wait_ge(s["place"], after(j))
                    for m in range(2):
                        pe.matmul(banks[m][:], cc[:, C_SEL + P * m:C_SEL + P * m + P], rd[:], start=True, stop=True)\
                          .then_inc(s["rb_psum"], 1)
                if f_on and t == T_WO:
                    for i in range(SUB):
                        for kc in range(KC):
                            pe.wait_ge(s["ot_ready"], after(2 * j + (kc + 1 if i == 0 else 2)))
                            mm = pe.matmul(banks[i // 2][:, D * (i % 2):D * (i % 2) + D],
                                           ot[:, kc, P * i:P * i + P], wo[:, kc, :], start=(kc == 0), stop=(kc == KC - 1))
                        if i % 2:
                            mm.then_inc(s["wo_psum"], 1)
                if a_on and t in T_MAX:
                    i = T_MAX.index(t)
                    for g in range(NG):
                        c = NG * i + g
                        if c == 0:
                            pe.wait_ge(s["kbm_loaded"], after(16 * (ba + 1)))
                        if c < 2:
                            pe.wait_ge(s["q_lo"], after(2 * (a + 1)))
                        else:
                            pe.wait_ge(s["max_read"], after(SUB * NG * a + c - 1))
                        pe.matmul(banks[2 + c % 2][:, 0:GROWS], qh[:, g // 2, P * i:P * i + P],
                                  kbm[:, g // 2, GROWS * (g % 2):GROWS * (g % 2) + GROWS],
                                  start=True, stop=True).then_inc(s["max_psum"], 1)
                if f_on and t == T_X2T:
                    for h in range(KC):
                        for i in range(SUB):
                            pe.wait_ge(s["x2_ready"], after(SUB * j + i + 1))
                            mm = pe.transpose(banks[h][:, P * i:P * i + P], row[:, v, i, P * h:P * h + P], ident)
                        mm.then_inc(s["x2t_psum"], 1)
                if f_on and t == T_LOGITS:
                    pe.wait_ge(s["x2t_ready"], after(KC * (j + 1)))
                    for i in range(SUB):
                        for kc in range(KC):
                            mm = pe.matmul(banks[0][:, E * i:E * i + E], x2t[:, kc, P * i:P * i + P], wgs[:, kc, :],
                                           start=(kc == 0), stop=(kc == KC - 1))
                    mm.then_inc(s["lg_psum"], 1)
                if a_on and t == T_NEGMAX:
                    pe.wait_ge(s["negmax"], after(a + 1))
                    for i in range(SUB):
                        mm = pe.transpose(banks[2][0:H, P * i:P * i + P], nm[:, i, :], ident)
                    mm.then_inc(s["nmt_psum"], 1)
                if f_on and t == T_POS:
                    pe.wait_ge(s["bothb_ready"], after(j + 1))
                    pe.wait_ge(s["carryb_ready"], after(j + 1))
                    for i in range(SUB):
                        o = banks[1][:, E * i:E * i + E]
                        pe.matmul(o, tri[:], bothb[:, i, :], start=True, stop=False)
                        for before in range(i):
                            pe.matmul(o, ones[:], bothb[:, before, :], start=False, stop=False)
                        mm = pe.matmul(o, ones[:], carryb[:], start=False, stop=True)
                    mm.then_inc(s["pos_psum"], 1)
            if b_on:
                pe_values(pe, k, n, NT - 2)
                pe_values(pe, k, n, NT - 1)

        @block.tensor
        def _(pe):
            steps(pe, pe_step)

        def act_group(act, k, g):
            act.wait_ge(s["pv_tile"], after(NT * k + 3 * g + 3))
            act.wait_ge(s["ot_ready"], after(2 * k))
            act.activation(ou[64 * (g % 2):64 * (g % 2) + 64, g // 2, :], PV[g % 2][0:64, :], ACT.Copy)\
               .then_inc(s["ou_ready"], 1)
            act.wait_ge(s["rd_ready"], after(k))
            act.activation(dt[32 * g:32 * g + 32, :], PV[g % 2][64:96, :], ACT.Copy).then_inc(s["dt_ready"], 1)

        def act_step(act, k, u, n, ln_on, a_on, b_on, f_on):
            a, j, v = k + 1, k - 1, 1 - u
            if not a_on and not f_on:
                keep_keys(act, 64, kbh, s_kept)
            for t in range(NT):
                if b_on:
                    w = TL[t % 3]
                    act.wait_ge(s["sc_psum"], after(NT * k + t + 1))
                    act.wait_ge(s["pv_tile"], after(NT * k + t - NP + 1))
                    act.activation(pr[0:w, t % NP, :], SC[t % 2][0:w, :], ACT.Exp, scale=SCALE).then_inc(s["p_ready"], 1)
                    if t in (5, 8, 11):
                        act_group(act, k, (t - 5) // 3)
                if a_on and t == T_XT:
                    act.wait_ge(s["q_psum"], after(2 * a))
                    for h in range(KC):
                        act.wait_ge(s["xt_psum"], after(KC * a + h + 1))
                        act.activation(xT[:, h, :], banks[2 + h][:], ACT.Copy).then_inc(s["xt_ready"], 1)
                if a_on and t == T_Q:
                    act.wait_ge(s["max_psum"], after(SUB * NG * a))
                    act.wait_ge(q_stacked[u], after(QS * (n + 1)))
                    for m in range(2):
                        act.wait_ge(s["q_psum"], after(2 * a + m + 1))
                        act.activation(qh[:, m, :], banks[2 + m][:], ACT.Identity, bias=bc[:, 0, m:m + 1])\
                           .then_inc(s["q_hi"], 1)
                if f_on and t == T_X2T:
                    act.wait_ge(s["lg_psum"], after(j))
                    for h in range(KC):
                        act.wait_ge(s["x2t_psum"], after(KC * j + h + 1))
                        act.activation(x2t[:, h, :], banks[h][:], ACT.Copy).then_inc(s["x2t_ready"], 1)
                if a_on and t == T_NEGMAX:
                    act.wait_ge(s["nmt_psum"], after(a + 1))
                    act.activation(nmt[:], banks[2][0:H, :], ACT.Copy).then_inc(s["nmt_ready"], 1)
                if f_on and t == T_EX:
                    act.wait_ge(s["dif_ready"], after(j + 1))
                    act.wait_ge(s["gate1"], after(j))
                    act.activation(ex[:], dif[:], ACT.Exp).then_inc(s["ex_ready"], 1)
            if b_on:
                act_group(act, k, NG - 1)

        @block.scalar
        def _(act):
            steps(act, act_step)

        def statistics(dve, src, c, stats, name, first):
            for i in range(SUB):
                first(i)
                dve.wait_ge(s[name + "_mv"], after(SUB * c))
                dve.bn_stats(stats[:, i, :], src[:, i, :]).then_inc(s[name + "_stats"], 1)

        def aggregate(dve, c, stats, moments, name):
            dve.wait_ge(s[name + "_ready"], after(SUB * c))
            dve.wait_ge(s[name + "_stats"], after(SUB * (c + 1)))
            dve.sem_inc(passed["dve"], 1)
            for i in range(SUB):
                dve.bn_aggr(moments[:, i, :], stats[:, i, :]).then_inc(s[name + "_mv"], 1)

        def maxima(dve, a, i):
            for g in range(NG):
                c = NG * i + g
                dve.wait_ge(s["max_psum"], after(SUB * NG * a + c + 1))
                dve.tensor_reduce(mx[:, i, GH * g:GH * g + GH],
                                  banks[2 + c % 2][:, 0:GROWS].rearrange("p (h s) -> p h s", h=GH),
                                  AX_X, ALU.max).then_inc(s["max_read"], 1)

        def dve_step(dve, k, u, n, ln_on, a_on, b_on, f_on):
            a, j, v = k + 1, k - 1, 1 - u
            if f_on:
                dve.wait_ge(s["dt_ready"], after(NG * (j + 1)))
                dve.wait_ge(s["rb_psum"], after(2 * j))
                dve.reciprocal(rd[:], dt[:]).then_inc(s["rd_ready"], 1)
            if a_on:
                dve.wait_ge(q_stacked[u], after(QS * (n + 1)))
                for m in range(2):
                    dve.wait_ge(s["q_hi"], after(2 * a + m + 1))
                    dve.scalar_tensor_tensor(out=ql[:, m, :], in0=banks[2 + m][:], scalar=bc[:, 0, m:m + 1],
                                             in1=qh[:, m, :], op0=ALU.add, op1=ALU.subtract).then_inc(s["q_lo"], 1)
            if f_on:
                dve.wait_ge(s["ou_ready"], after(NG * (j + 1)))
                dve.wait_ge(s["wo_psum"], after(2 * j))
                for m in range(2):
                    dve.wait_ge(s["rb_psum"], after(2 * j + m + 1))
                    dve.tensor_tensor(ot[:, m, :], banks[m][:], ou[:, m, :], ALU.mult).then_inc(s["ot_ready"], 1)
            if a_on:
                dve.wait_ge(s["negmax"], after(a))
                maxima(dve, a, 0)
            if f_on:
                dve.wait_ge(s["xr_bias"], after(j + 1))
                dve.wait_ge(s["x1_stored"], after(16 * j))
                dve.wait_ge(s["x2_ready"], after(SUB * j))
                for m in range(2):
                    dve.wait_ge(s["wo_psum"], after(2 * j + m + 1))
                    for i in range(2 * m, 2 * m + 2):
                        dve.tensor_tensor(x1[:, i, :], banks[m][:, D * (i % 2):D * (i % 2) + D], xr[:, i, :],
                                          ALU.add).then_inc(s["x1_ready"], 1)
            if a_on:
                maxima(dve, a, 1)
            if f_on:
                statistics(dve, x1, j, st2, "x2", lambda i: dve.wait_ge(s["x1_ready"], after(SUB * j + i + 1)))
                aggregate(dve, j, st2, mv2, "x2")
            if a_on:
                maxima(dve, a, 2)
                maxima(dve, a, 3)
                dve.wait_ge(s["max_read"], after(SUB * NG * (a + 1)))
                dve.wait_ge(s["nmt_psum"], after(a))
                dve.tensor_scalar(nm[:], mx[:], -1.0, None, ALU.mult).then_inc(s["negmax"], 1)
            if f_on:
                dve.wait_ge(s["x2_rs"], after(j + 1))
                dve.wait_ge(s_scat[v], after(16 * SUB * TOPK * n, 16))
                for i in range(SUB):
                    dve.tensor_scalar(row[:, v, i, 0:D], x1[:, i, :], mv2[:, i, 0:1], rs2[:, i:i + 1],
                                      ALU.subtract, ALU.mult).then_inc(s["x2_ready"], 1)
                dve.wait_ge(s["tok_ready"], after(j + 1))
                dve.tensor_copy(row[:].bitcast(I32)[:, v, :, D], tok[:]).then_inc(s["tok_row"], 1)
            if ln_on:
                dve.wait_ge(s["x_loaded"], after(16 * (a + 2)))
                statistics(dve, xt, a + 1, st, "xn", lambda i: None)
                aggregate(dve, a + 1, st, mv, "xn")
            if f_on:
                dve.wait_ge(s["tok_row"], after(j + 1))
                dve.tensor_scalar(tok[:], tok[:], CH, None, ALU.add).then_inc(s["tok_ready"], 1)
                choose(dve, j)
            if ln_on:
                dve.wait_ge(s["xn_rs"], after(a + 2))
                dve.wait_ge(s["xt_psum"], after(KC * (a + 1)))
                for i in range(SUB):
                    dve.tensor_scalar(xn[:, i, :], xt[:, i, :], mv[:, i, 0:1], rs[:, i:i + 1],
                                      ALU.subtract, ALU.mult).then_inc(s["xn_ready"], 1)
            if f_on:
                route(dve, j, v)

        def choose(dve, j):
            dve.wait_ge(s["dif_ready"], after(j))
            dve.wait_ge(s["idx_ready"], after(SUB * j))
            dve.wait_ge(s["lg_psum"], after(j + 1))
            dve.sem_inc(passed["dve"], 1)
            for i in range(SUB):
                dve.max(top8[:, i, :], banks[0][:, E * i:E * i + E]).then_inc(s["top_ready"], 1)
            dve.wait_ge(s["idf_ready"], after(j))
            for i in range(SUB):
                dve.wait_ge(s["top_ready"], after(SUB * j + i + 1))
                dve.sem_inc(passed["dve"], 1)
                dve.max_index(idx8[:, i, :], top8[:, i, :], banks[0][:, E * i:E * i + E]).then_inc(s["idx_ready"], 1)
            dve.wait_ge(s["ex_ready"], after(j))
            dve.tensor_tensor(dif[:], top8[:, :, 1], top8[:, :, 0], ALU.subtract).then_inc(s["dif_ready"], 1)
            dve.wait_ge(s["idx_ready"], after(SUB * (j + 1)))
            dve.wait_ge(s["oh_ready"], after(j))
            dve.tensor_copy(idf[:], idx8[:, :, 0:TOPK].rearrange("p i r -> p r i")).then_inc(s["idf_ready"], 1)
            dve.wait_ge(s["idf_ready"], after(j + 1))
            dve.wait_ge(s["pk_ready"], after(j))
            dve.wait_ge(s["gw_ready"], after(j))
            dve.wait_ge(s["bothb_ready"], after(j))
            pairs = lambda ap: ap.rearrange("p r i -> p (r i)").rearrange("p (c a) -> p c a", a=1)
            flat = lambda ap: ap.rearrange("p r i e -> p (r i) e")
            dve.tensor_tensor(flat(oh[:]), cc[:, C_IO:C_IO + 64].rearrange("p (c e) -> p c e", e=E),
                              bcast(pairs(idf[:]), [P, TOPK * SUB, E]), ALU.is_equal).then_inc(s["oh_ready"], 1)
            dve.wait_ge(s["oh_ready"], after(j + 1))
            dve.wait_ge(s["pos_psum"], after(j))
            dve.wait_ge(s["chosen"], after(j))
            dve.tensor_tensor(bothb[:], oh[:, 0], oh[:, 1], ALU.add).then_inc(s["bothb_ready"], 1)

        def route(dve, j, v):
            pairs = lambda ap: ap.rearrange("p r i -> p (r i)").rearrange("p (c a) -> p c a", a=1)
            flat = lambda ap: ap.rearrange("p r i e -> p (r i) e")
            dve.wait_ge(s["ex_ready"], after(j + 1))
            dve.wait_ge(s["gate0"], after(j))
            dve.tensor_scalar(den[:], ex[:], 1.0, None, ALU.add).then_inc(s["den_ready"], 1)
            dve.wait_ge(s["bothb_ready"], after(j + 1))
            dve.wait_ge(s["carry_ready"], after(j + 1))
            dve.tensor_reduce(chosen[:], bothb[:].rearrange("p i e -> p e i"), AX_X, ALU.add).then_inc(s["chosen"], 1)
            dve.wait_ge(s["den_ready"], after(j + 1))
            dve.wait_ge(s["gw_ready"], after(j))
            dve.reciprocal(gate[:, 0], den[:]).then_inc(s["gate0"], 1)
            dve.wait_ge(s["chosen"], after(j + 1))
            dve.wait_ge(s["carryb_ready"], after(j + 1))
            dve.tensor_tensor(carry[:], carry[:], chosen[:], ALU.add).then_inc(s["carry_ready"], 1)
            dve.wait_ge(s["gate0"], after(j + 1))
            dve.tensor_tensor(gate[:, 1], gate[:, 0], ex[:], ALU.mult).then_inc(s["gate1"], 1)
            dve.wait_ge(s["gate1"], after(j + 1))
            dve.wait_ge(s["gate_row"], after(j))
            dve.tensor_tensor(flat(gw[:]), flat(oh[:]), bcast(pairs(gate[:]), [P, TOPK * SUB, E]), ALU.mult)\
               .then_inc(s["gw_ready"], 1)
            dve.wait_ge(s["pos_psum"], after(j + 1))
            dve.wait_ge(s["place"], after(j))
            ranks = banks[1][:, 0:SUB * E].rearrange("p (i e) -> p i e", e=E)
            dve.tensor_tensor(over[:], ranks, cc[:, C_EB:C_EB + 32].rearrange("p (i e) -> p i e", e=E),
                              ALU.is_ge).then_inc(s["over"], 1)
            dve.wait_ge(s["gw_ready"], after(j + 1))
            dve.tensor_tensor(row[:, v, :, D + 1:ROW], gw[:, 0], gw[:, 1], ALU.add).then_inc(s["gate_row"], 1)
            dve.wait_ge(s["over"], after(j + 1))
            dve.wait_ge(s["pk_ready"], after(j))
            dve.scalar_tensor_tensor(out=place[:], in0=over[:], scalar=BIG, in1=ranks, op0=ALU.mult, op1=ALU.add)\
               .then_inc(s["place"], 1)
            dve.wait_ge(s["carry_ready"], after(j + 2))
            dve.tensor_copy(carryb[:], carry[:]).then_inc(s["carryb_ready"], 1)
            dve.wait_ge(s["place"], after(j + 1))
            dve.wait_ge(s["destf_ready"], after(j))
            dve.tensor_tensor(pk[:], oh[:], bcast(place[:].rearrange("p (a i) e -> p a i e", a=1), [P, TOPK, SUB, E]),
                              ALU.mult).then_inc(s["pk_ready"], 1)
            dve.wait_ge(s["pk_ready"], after(j + 1))
            dve.wait_ge(s["dest_ready"], after(j))
            dve.tensor_reduce(destf[:], flat(pk[:]), AX_X, ALU.add).then_inc(s["destf_ready"], 1)
            dve.wait_ge(s["destf_ready"], after(j + 1))
            dve.tensor_copy(dest[:, v].rearrange("p r i -> p (r i)"), destf[:]).then_inc(s["dest_ready"], 1)

        @block.vector
        def _(dve):
            dve.tensor_copy(carry[:], cc[:, C_START:C_START + E]).then_inc(s["carry_ready"], 1)
            dve.wait_ge(s["carry_ready"], after(1))
            dve.tensor_copy(carryb[:], carry[:]).then_inc(s["carryb_ready"], 1)
            steps(dve, dve_step)

        def scatter(pool, u, c):
            i, r = c // TOPK, c % TOPK
            pool.indirect_dma_start(
                slots[:, :], bass.IndirectOffsetOnAxis(ap=dest[:].bitcast(U32)[:, u, r, i:i + 1], axis=0),
                row[:, u, i, :], None, bounds_check=E * CAP - 1, oob_is_err=False).then_inc(s_scat[u], 16)

        def pool_step(pool, k, u, n, ln_on, a_on, b_on, f_on):
            a, j = k + 1, k - 1
            if f_on:
                pool.wait_ge(s_init, 16 * FILLS)
                pool.wait_ge(s["tok_row"], after(j))
                pool.wait_ge(s["gate_row"], after(j))
                pool.wait_ge(s["dest_ready"], after(j))
                pool.sem_inc(passed["pool"], 1)
                for c in range(2):
                    scatter(pool, u, c)
                pool.wait_ge(s["xr_loaded"], after(16 * (j + 1)))
                pool.tensor_tensor(xr[:], xr[:], bcast(bo_row[:].rearrange("p (a d) -> p a d", a=1), [P, SUB, D]),
                                   ALU.add).then_inc(s["xr_bias"], 1)
                for c in range(2, SUB * TOPK):
                    scatter(pool, u, c)
                variance_root(pool, j, mv2, ve2, rs2, "x2")
            if ln_on:
                variance_root(pool, a + 1, mv, ve, rs, "xn")
            if not a_on and not f_on:
                keep_keys(pool, 32, kbl, s_kept_low)

        def variance_root(pool, c, moments, plus, root, name):
            pool.wait_ge(s[name + "_rs"], after(c))
            pool.wait_ge(s[name + "_mv"], after(SUB * (c + 1)))
            pool.sem_inc(passed["pool"], 1)
            pool.tensor_scalar(plus[:], moments[:, :, 1], EPS, None, ALU.add).then_inc(s[name + "_ve"], 1)
            pool.wait_ge(s[name + "_ve"], after(c + 1))
            pool.wait_ge(s[name + "_ready"], after(SUB * c))
            pool.tensor_tensor(root[:], plus[:], half[:], ALU.pow).then_inc(s[name + "_rs"], 1)

        @block.gpsimd
        def _(pool):
            pool.iota(tok[:], pattern=[[P, SUB]], base=0, channel_multiplier=1).then_inc(s["tok_ready"], 1)
            pool.memset(half[:], -0.5).then_inc(s["pool_set"], 1)
            pool.memset(row[:, 1], 0.0).then_inc(s["pool_set"], 1)
            pool.memset(dest[:, 1], int(BIG)).then_inc(s["pool_set"], 1)
            pool.wait_ge(s["pool_set"], after(3))
            steps(pool, pool_step)
            pool.wait_ge(s["gate_row"], after(NCH))
            pool.wait_ge(s["dest_ready"], after(NCH))
            for c in range(SUB * TOPK):
                scatter(pool, 1, c)


def experts(nc, ctx, whole, passed, banks, slots, w1, b1, w2, b2, out):
    sb = lambda name, shape, dt: ctx.enter_context(nc.sbuf_tensor(name, shape, dt))
    ident = whole["cc"][:, C_ID:C_ID + P]
    w1raw, w2raw = whole["w1raw"], whole["w2raw"]
    MT = HID // P
    sizes = [[min(TT, CAP - XC * c - TT * t) for t in range(3)] for c in range(NX)]
    STEPS = NX * MT
    assert all(min(z) > 64 and sum(z) % 2 == 0 for z in sizes)

    w1h = [sb(f"w1h{i}", [P, KC, HID], F32R) for i in range(2)]
    w1l = [sb(f"w1l{i}", [P, KC, HID], F32R) for i in range(2)]
    w2h = [sb(f"w2h{i}", [P, MT, D], F32R) for i in range(2)]
    w2l = [sb(f"w2l{i}", [P, MT, D], F32R) for i in range(2)]
    b1s = sb("b1s", [P, E, MT], F32)
    b2r = sb("b2r", [TT, E, D], F32)
    xin = [sb(f"xin{i}", [TT, 3, ROW], F32) for i in range(NX)]
    gcol = [sb(f"gcol{i}", [TT, 3, 1], F32) for i in range(NX)]
    xh = sb("xh", [P, 2, KC, XC], F32R)
    xl = sb("xl", [P, 2, KC, XC], F32R)
    NH = 4
    hf = sb("hf", [P, NH, XC], F32)
    hh = sb("hh", [P, NH, XC], F32R)
    hl = sb("hl", [P, NH, XC], F32R)
    b2g = sb("b2g", [TT, 2, 3, D], F32)
    ys = sb("ys", [TT, 2, 3, D], F32)
    XT, HB, YB = banks[0:2], [banks[2], banks[3], banks[7]], banks[4:7]

    s, x_in, added, s_w = whole["e"], whole["x_in"], whole["added"], whole["s_w"]
    block = ctx.enter_context(nc.Block())

    def pairs(eng, turn):
        with eng.Fori(0, E // 2 - 1) as b:
            turn(eng, b, False)
        turn(eng, E // 2 - 1, True)

    def chunks(b, last):
        for eo in range(2):
            for c in range(NX):
                e = 2 * b + eo
                yield e, eo, c, NX * e + c, not (last and eo == 1 and c == NX - 1)

    def sync_pair(sp, b, last):
        for e, eo, c, q, _ in chunks(b, last):
            sp.wait_ge(added[c], after(48 * e, 16))
            lo, two, z = e * CAP + XC * c, 2 * TT, sizes[c][2]
            front = slots[bass.ds(lo, two), :].rearrange("(t p) r -> p t r", p=TT)
            sp.dma_start(xin[c][:, 0:2, :], front).then_inc(x_in[c], 16)
            sp.dma_start(xin[c][0:z, 2, :], slots[bass.ds(lo + two, z), :]).then_inc(x_in[c], 16)
            sp.dma_start(gcol[c][:, 0:2, :], slots[bass.ds(lo, two), bass.ds(D + 1 + e, 1)]
                         .rearrange("(t p) r -> p t r", p=TT), allow_slow_non_contiguous=True).then_inc(x_in[c], 16)
            sp.dma_start(gcol[c][0:z, 2, :], slots[bass.ds(lo + two, z), bass.ds(D + 1 + e, 1)],
                         allow_slow_non_contiguous=True).then_inc(x_in[c], 16)
            if c == 0 and not (last and eo == 1):
                sp.wait_ge(s["w_split"], after(2 * (e + 1)))
                sp.dma_start(w1raw[:], w1[e + 1]).then_inc(s_w, 16)
                sp.dma_start(w2raw[:], w2[e + 1]).then_inc(s_w, 16)

    @block.sync
    def _(sp):
        sp.dma_start(b1s[:], b1).then_inc(s["b1_loaded"], 16)
        for u in range(2):
            sp.wait_ge(whole["s_scat"][u], after(16 * SUB * TOPK * (NCH // 2 + u), 16))
        pairs(sp, sync_pair)

    def transpose_x(pe, e, c, q):
        pe.wait_ge(x_in[c], after(64 * (e + 1)))
        for kc in range(KC):
            for t, z in enumerate(sizes[c]):
                mm = pe.transpose(XT[kc][:, TT * t:TT * t + z], xin[c][0:z, t, P * kc:P * kc + P], ident[0:z, 0:z])
            mm.then_inc(s["xt_psum"], 1)

    def layer1(pe, e, eo, c, q, m):
        n, at, g = sum(sizes[c]), MT * c + m, STEPS * e + MT * c + m
        o = HB[at % 3][:, 0:n]
        if m == 0:
            pe.wait_ge(s["xt_low"], after(KC * (q + 1)))
            if c == 0:
                pe.wait_ge(s["w_split"], after(2 * e + 1))
        if eo or at >= 3:
            pe.wait_ge(s["h_full"], after(g - 2))
        x0 = (NX * eo + c) % 2
        k = 0
        for w_, x_ in ((w1h, xh), (w1h, xl), (w1l, xh)):
            for kc in range(KC):
                mm = pe.matmul(o, w_[eo][:, kc, P * m:P * m + P], x_[:, x0, kc, 0:n], start=(k == 0), stop=(k == 5))
                k += 1
        mm.then_inc(s["h_psum"], 1)

    def layer2(pe, e, eo, c, q, m):
        g = STEPS * e + MT * c + m
        if m == 0:
            if c == 0:
                pe.wait_ge(s["w_split"], after(2 * e + 2))
        pe.wait_ge(s["h_low"], after(g + 1))
        for t, z in enumerate(sizes[c]):
            if m == 0:
                pe.wait_ge(s["y_ready"], after(3 * (q - 1) + t + 1 if eo or c else 3 * q))
            for h_, w_ in ((hh, w2h), (hh, w2l), (hl, w2h)):
                first, final = m == 0 and h_ is hh and w_ is w2h, m == MT - 1 and h_ is hl
                mm = pe.matmul(YB[t][0:z, 0:D], h_[:, m % NH, TT * t:TT * t + z], w_[eo][:, m, :],
                               start=first, stop=final)
        mm.then_inc(s["l2_done"], 1)

    def pe_pair(pe, b, last):
        behind = []
        for e, eo, c, q, follows in chunks(b, last):
            for m in range(MT):
                layer1(pe, e, eo, c, q, m)
                behind.append((e, eo, c, q, m))
                for _ in range(0 if m == 2 else 2 if m == 5 else 1):
                    if len(behind) > 2:
                        layer2(pe, *behind.pop(0))
                if m == 4 and follows:
                    transpose_x(pe, e + (c == NX - 1), (c + 1) % NX, q + 1)
        for one in behind:
            layer2(pe, *one)

    @block.tensor
    def _(pe):
        transpose_x(pe, 0, 0, 0)
        pairs(pe, pe_pair)

    def round_x(act, c, q, x0):
        n = sum(sizes[c])
        act.wait_ge(s["h_psum"], after(MT * (q - 1)))
        for kc in range(KC):
            act.wait_ge(s["xt_psum"], after(KC * q + kc + 1))
            act.activation(xh[:, x0, kc, 0:n], XT[kc][:, 0:n], ACT.Copy).then_inc(s["xt_high"], 1)

    def act_pair(act, b, last):
        for e, eo, c, q, follows in chunks(b, last):
            n = sum(sizes[c])
            for m in range(MT):
                at, g = MT * c + m, STEPS * e + MT * c + m
                act.wait_ge(s["l2_done"], after(STEPS * e if not eo and at < NH else g - NH + 1))
                act.wait_ge(s["h_psum"], after(g + 1))
                act.sem_inc(passed["act"], 1)
                for h_, ready in ((hh, "h_high"), (hf, "h_full")):
                    act.activation(h_[:, m % NH, 0:n], HB[at % 3][:, 0:n], ACT.Gelu_apprx_tanh,
                                   bias=b1s[:, e, m:m + 1]).then_inc(s[ready], 1)
                if m == 4 and follows:
                    round_x(act, (c + 1) % NX, q + 1, (NX * eo + c + 1) % 2)

    @block.scalar
    def _(act):
        act.wait_ge(s["b1_loaded"], after(16))
        round_x(act, 0, 0, 0)
        pairs(act, act_pair)

    def split_weights(dve, e, eo, part):
        raw, high, low = ((w1raw, w1h, w1l), (w2raw, w2h, w2l))[part // 2]
        if part % 2 == 0:
            dve.wait_ge(s_w, after(32 * (e + 1)))
            dve.wait_ge(s["l2_done"], after(STEPS * (e - 1)))
            dve.tensor_copy(high[eo][:], raw[:]).then_inc(s["w_high"], 1)
        else:
            dve.wait_ge(s["w_high"], after(2 * e + part // 2 + 1))
            dve.tensor_tensor(low[eo][:], raw[:], high[eo][:], ALU.subtract).then_inc(s["w_split"], 1)

    def rest_x(dve, c, q, x0):
        n = sum(sizes[c])
        for kc in range(KC):
            dve.wait_ge(s["xt_high"], after(KC * q + kc + 1))
            dve.tensor_tensor(xl[:, x0, kc, 0:n], XT[kc][:, 0:n], xh[:, x0, kc, 0:n], ALU.subtract)\
               .then_inc(s["xt_low"], 1)

    def outputs(dve, e, eo, c, q):
        y0 = (NX * eo + c) % 2
        dve.wait_ge(s["l2_done"], after(MT * (q + 1)))
        dve.wait_ge(s["b2g_ready"], after(3 * (q + 1)))
        if c >= 2:
            dve.wait_ge(added[c - 2], after(48 * (e + 1), 16))
        else:
            dve.wait_ge(added[c + 1], after(48 * e, 16))
        for t, z in enumerate(sizes[c]):
            dve.scalar_tensor_tensor(out=ys[0:z, y0, t, :], in0=YB[t][0:z, 0:D], scalar=gcol[c][0:z, t, :],
                                     in1=b2g[0:z, y0, t, :], op0=ALU.mult, op1=ALU.add).then_inc(s["y_ready"], 1)

    def dve_pair(dve, b, last):
        behind = None
        for e, eo, c, q, follows in chunks(b, last):
            n = sum(sizes[c])
            for m in range(MT):
                g = STEPS * e + MT * c + m
                dve.wait_ge(s["h_full"], after(g + 1))
                dve.tensor_tensor(hl[:, m % NH, 0:n], hf[:, m % NH, 0:n], hh[:, m % NH, 0:n], ALU.subtract)\
                   .then_inc(s["h_low"], 1)
                if m == 1 and behind:
                    outputs(dve, *behind)
                if c == 1 and m % 2 and not (last and eo == 1):
                    split_weights(dve, e + 1, 1 - eo, m // 2)
                if m == 4 and follows:
                    rest_x(dve, (c + 1) % NX, q + 1, (NX * eo + c + 1) % 2)
            behind = (e, eo, c, q)
        outputs(dve, *behind)

    @block.vector
    def _(dve):
        for part in range(4):
            split_weights(dve, 0, 0, part)
        rest_x(dve, 0, 0, 0)
        pairs(dve, dve_pair)

    def pool_pair(pool, b, last):
        for e, eo, c, q, _ in chunks(b, last):
            y0 = (NX * eo + c) % 2
            pool.wait_ge(s["y_ready"], after(3 * q))
            pool.wait_ge(x_in[c], after(64 * (e + 1)))
            pool.sem_inc(passed["pool"], 1)
            for t, z in enumerate(sizes[c]):
                pool.tensor_tensor(b2g[0:z, y0, t, :], b2r[0:z, e, :], gcol[c][0:z, t, :].to_broadcast([z, D]),
                                   ALU.mult).then_inc(s["b2g_ready"], 1)
            for t, z in enumerate(sizes[c]):
                if t:
                    pool.wait_ge(added[c], after(48 * e + 16 * t, 16))
                elif c:
                    pool.wait_ge(added[c - 1], after(48 * (e + 1), 16))
                else:
                    pool.wait_ge(added[NX - 1], after(48 * e, 16))
                pool.wait_ge(s["y_ready"], after(3 * q + t + 1))
                pool.sem_inc(passed["pool"], 1)
                pool.indirect_dma_start(
                    out[:, :], bass.IndirectOffsetOnAxis(ap=xin[c][0:z, t, D:D + 1].bitcast(U32), axis=0),
                    ys[0:z, y0, t, :], None, bounds_check=NTOK - 1, oob_is_err=False,
                    compute_op=ALU.add).then_inc(added[c], 16)

    @block.gpsimd
    def _(pool):
        part = TT // NX
        for c in range(NX):
            pool.dma_start(b2r[part * c:part * c + part], b2[:, :].rearrange("(a e) d -> a e d", a=1)
                           .to_broadcast([part, E, D])).then_inc(added[c], 16)
        for c in range(NX):
            pool.wait_ge(added[c], 16)
        pairs(pool, pool_pair)
        for c in range(NX):
            pool.wait_ge(added[c], after(48 * E, 16))


def kernel(**inputs):
    import numpy as np
    import concourse.bacc as bacc
    from concourse.bass_utils import run_bass_kernel_spmd

    a = {k: np.asarray(v) for k, v in inputs.items()}
    g = lambda name: a["L0_" + name]
    rows = lambda w: w.reshape(-1, P, w.shape[-1]).transpose(1, 0, 2)
    columns = lambda v: v.reshape(-1, P).T
    arrays = {
        "x": a["x"].reshape(NTOK, D),
        "ctxT": rows(a["ctx_1024"].reshape(B * S, D).T),
        "watt": np.stack([rows(g("xattn_W" + n)) for n in "kvqo"], axis=1),
        "wg": rows(g("ffn_Wg")),
        "bcols": np.stack([columns(g("xattn_b" + n)) for n in "qk"], axis=1),
        "brows": np.stack([g("xattn_bv"), g("xattn_bo")]),
        "w1": g("ffn_W1").reshape(E, KC, P, HID).transpose(0, 2, 1, 3),
        "b1": g("ffn_b1").reshape(E, HID // P, P).transpose(2, 0, 1),
        "w2": g("ffn_W2").reshape(E, HID // P, P, D).transpose(0, 2, 1, 3),
        "b2": g("ffn_b2"),
        "cst": constants(np),
    }
    arrays = {k: np.ascontiguousarray(v) for k, v in arrays.items()}
    nc = bacc.Bacc("TRN2", target_bir_lowering=False, num_devices=1)
    aps = {k: nc.dram_tensor(k, v.shape, F32, kind="ExternalInput").ap() for k, v in arrays.items()}
    out = nc.dram_tensor("out", (NTOK, D), F32, kind="ExternalOutput").ap()
    build(nc, out=out, **aps)
    r = run_bass_kernel_spmd(nc, [arrays], core_ids=[0])
    return r.results[0]["out"].reshape(B, L, D)
```

```python
from contextlib import ExitStack

import concourse.bass as bass
from concourse import mybir
from concourse.alu_op_type import AluOpType as ALU

F32 = mybir.dt.float32
F32R = mybir.dt.float32r
BF16 = mybir.dt.bfloat16
I32 = mybir.dt.int32
U32 = mybir.dt.uint32
ACT = mybir.ActivationFunctionType
AX_X = mybir.AxisListType.X

P = 128
B, L, D = 4, 1024, 256
S, H = 77, 16
HD = D // H
SCALE = HD ** -0.5
EPS = 1e-5
E, HID, TOPK = 8, 1024, 2
NTOK = B * L
CAP = -(-NTOK * TOPK * 105 // (E * 100))
CH = 512
NCH = NTOK // CH
SUB = CH // P
KC = D // P
GH = 4
NG = H // GH
GROWS = GH * S
TL = [104, 102, 102]
TO = [0, 104, 206]
TW = max(TL)
NT = NG * len(TL)
TT = 120
XC = 3 * TT
NX = -(-CAP // XC)
ROW = D + E
BIG = 100000.0
KROWS = 3 * 2 * HD + H


T_Q, T_NEGMAX = 1, 8
T_MAX = (3, 3, 4, 4, 5, 6, 7, 7)
T_SPREAD, T_WO, T_X2T, T_LOGITS, T_EX, T_POS = 2, 3, 8, 9, 10, 11


def segments():
    out = []
    for hl in range(GH):
        for j in range(len(TL)):
            lo, hi = max(hl * S, TO[j]), min((hl + 1) * S, TO[j] + TL[j])
            if lo < hi:
                out.append((hl, j, lo - TO[j], lo - hl * S, hi - lo))
    return out


C_ID = 0
C_TRI = C_ID + P
C_SEL = C_TRI + P
C_BLK = C_SEL + 2 * P
C_ON = C_BLK + 8 * S
C_OH = C_ON + 3 * P
C_IO = C_OH + NT * TW
C_EB = C_IO + TOPK * SUB * E
C_START = C_EB + SUB * E
C_N = C_START + E


def constants(np):
    c = np.zeros((P, C_N), np.float32)
    c[:, C_ID:C_ID + P] = np.eye(P)
    c[:, C_TRI:C_TRI + P] = np.triu(np.ones((P, P)), 1)
    for g in range(NG):
        for hl in range(GH):
            at = C_SEL + (g // 2) * P + 64 * (g % 2) + HD * hl
            c[32 * g + 8 * hl, at:at + HD] = 1
    for h in range(8):
        c[HD * h:HD * h + HD, C_BLK + S * h:C_BLK + S * h + S] = 1
    for hl, j, p0, _, n in segments():
        c[p0:p0 + n, C_ON + P * j + 64 + 8 * hl:C_ON + P * j + 64 + 8 * hl + 8] = 1
        for g in range(NG):
            t = 3 * g + j
            c[96 + GH * g + hl, C_OH + TW * t + p0:C_OH + TW * t + p0 + n] = 1
    c[:, C_IO:C_IO + TOPK * SUB * E] = np.tile(np.arange(E), TOPK * SUB)
    c[:, C_EB:C_EB + SUB * E] = np.tile(np.arange(E) * CAP + CAP, SUB)
    for e in range(E):
        c[:, C_START + e] = [(e * CAP * (p + 1)) // P - (e * CAP * p) // P for p in range(P)]
    return c


COUNTS = """xn_stats xn_mv xn_ve xn_rs xn_ready xt_psum xt_ready q_psum q_hi q_lo max_psum max_read negmax
    nmt_psum nmt_ready sc_psum p_ready pv_tile ou_ready dt_ready rd_ready rb_psum ot_ready wo_psum
    xr_bias x1_ready x1_stored x2_stats x2_mv x2_ve x2_rs x2_ready tok_ready x2t_psum x2t_ready lg_psum
    top_ready idx_ready idf_ready dif_ready ex_ready den_ready gate0 gate1 oh_ready gw_ready gate_row
    bothb_ready chosen carry_ready carryb_ready pos_psum over place pk_ready destf_ready dest_ready
    tok_row x_loaded xr_loaded kbm_loaded k_loaded0 k_loaded1 v_loaded0 v_loaded1 pool_set""".split()
EXPERT_COUNTS = """w_high w_split b1_loaded xt_psum xt_high xt_low h_psum h_high h_full h_low x_clear l2_done
    table b2g_ready y_ready""".split()


def prime(eng, semaphores):
    for one in semaphores:
        eng.sem_inc(one, 1)


def after(count, primed=1):
    return (max(count, 0) if isinstance(count, int) else count) + primed


def scatter(pool, whole, slot_token, u, c):
    i, r = c // TOPK, c % TOPK
    pool.indirect_dma_start(
        slot_token[:, :], bass.IndirectOffsetOnAxis(ap=whole["dest"][:].bitcast(U32)[:, u, r, i:i + 1], axis=0),
        whole["number"][:, u, i:i + 1], None, bounds_check=E * CAP - 1, oob_is_err=False)\
        .then_inc(whole["s_scat"][u], 16)


def build(nc, x, ctxT, watt, wg, bcols, brows, w1, b1, w2, b2, cst, out):
    slot_token = nc.dram_tensor("slot_token", (E * CAP, 1), I32, kind="Internal").ap()
    rows = nc.dram_tensor("rows", (NTOK, ROW), F32, kind="Internal").ap()
    with ExitStack() as top:
        sb = lambda name, shape, dt: top.enter_context(nc.sbuf_tensor(name, shape, dt))
        sem = lambda name: top.enter_context(nc.semaphore(name))
        whole = dict(
            cc=sb("cc", [P, C_N], F32), number=sb("number", [P, 2, SUB], I32), dest=sb("dest", [P, 2, TOPK, SUB], I32),
            w1raw=sb("w1raw", [P, KC, HID], F32), w2raw=sb("w2raw", [P, HID // P, D], F32),
            b2r=sb("b2r", [TT, E, D], F32),
            row_stored=[sem(f"s_row_stored{u}") for u in range(2)], s_scat=[sem(f"s_scat{u}") for u in range(2)],
            s={n: sem("s_" + n) for n in COUNTS}, q_stacked=[sem(f"s_q_stacked{u}") for u in range(2)],
            e={n: sem("e_" + n) for n in EXPERT_COUNTS}, s_w=sem("e_weights"),
            x_in=[sem(f"e_x_in{i}") for i in range(NX)],
            tok_in=[sem(f"e_tok_in{i}") for i in range(NX)], added=[sem(f"e_added{i}") for i in range(NX)])
        passed = {n: sem("passed_" + n) for n in ("act", "dve", "pool")}
        banks = [top.enter_context(nc.psum_tensor(f"bank{i}", [P, 512], F32)) for i in range(8)]
        with ExitStack() as att:
            attention_and_routing(nc, att, whole, passed, banks, slot_token, rows,
                                  x, ctxT, watt, wg, bcols, brows, w1, w2, b2, cst, out)
        with ExitStack() as ffn:
            experts(nc, ffn, whole, passed, banks, slot_token, rows, w1, b1, w2, b2, out)


def attention_and_routing(nc, ctx, whole, passed, banks, slot_token, rows,
                          x, ctxT, watt, wg, bcols, brows, w1, w2, b2, cst, out):
    sb = lambda name, shape, dt: ctx.enter_context(nc.sbuf_tensor(name, shape, dt))
    sem = lambda name: ctx.enter_context(nc.semaphore(name))
    cc, s_scat, row_stored = whole["cc"], whole["s_scat"], whole["row_stored"]
    s, q_stacked = whole["s"], whole["q_stacked"]
    ident = cc[:, C_ID:C_ID + P]

    wq = sb("wq", [P, KC, D], F32)
    wo = sb("wo", [P, KC, D], F32)
    wgs = sb("wgs", [P, KC, E], F32)
    bc = sb("bc", [P, 2, KC], F32)
    bo_row = sb("bo_row", [P, D], F32)
    tri = sb("tri", [P, P], BF16)
    ones = sb("ones", [P, P], BF16)
    kst = sb("kst", [KROWS, NT, TW], F32R)
    vst = sb("vst", [TW, NT, P], F32)
    vf = sb("vf", [S, B, D], F32)
    nobody = sb("nobody", [32, E * CAP // 32], I32)
    k_tiles = nc.dram_tensor("k_tiles", (B, P, NT, TW), F32, kind="Internal").ap()
    k_diag = nc.dram_tensor("k_diag", (B, P, 2 * 8 * S), F32, kind="Internal").ap()

    kbm = sb("kbm", [P, 2, 8 * S], F32R)
    xt = sb("xt", [P, SUB, D], F32)
    st = sb("st", [P, SUB, 6], F32)
    mv = sb("mv", [P, SUB, 2], F32)
    ve = sb("ve", [P, SUB], F32)
    rs = sb("rs", [P, SUB], F32)
    half = sb("half", [P, SUB], F32)
    xn = sb("xn", [P, SUB, D], F32)
    xT = sb("xT", [P, KC, CH], F32)
    qh = sb("qh", [P, 2, CH], F32R)
    ql = sb("ql", [P, 2, CH], F32R)
    mx = sb("mx", [P, SUB, H], F32)
    nm = sb("nm", [P, SUB, H], F32)
    nmt = sb("nmt", [H, CH], F32R)
    qs = sb("qs", [KROWS, 2, NT, CH], F32R)
    st2 = sb("st2", [P, SUB, 6], F32)
    mv2 = sb("mv2", [P, SUB, 2], F32)
    ve2 = sb("ve2", [P, SUB], F32)
    rs2 = sb("rs2", [P, SUB], F32)
    NP = 4
    pr = sb("pr", [TW, NP, CH], F32)
    ou = sb("ou", [P, 2, CH], F32)
    dt = sb("dt", [P, CH], F32)
    row = sb("row", [P, 2, SUB, ROW], F32)
    dest, number = whole["dest"], whole["number"]
    top8 = sb("top8", [P, SUB, 8], F32)
    idx8 = sb("idx8", [P, SUB, 8], U32)
    idf = sb("idf", [P, TOPK, SUB], F32)
    dif = sb("dif", [P, SUB], F32)
    ex = sb("ex", [P, SUB], F32)
    den = sb("den", [P, SUB], F32)
    gate = sb("gate", [P, TOPK, SUB], F32)
    oh = sb("oh", [P, TOPK, SUB, E], F32)
    gw = sb("gw", [P, TOPK, SUB, E], F32)
    bothb = sb("bothb", [P, SUB, E], BF16)
    chosen = sb("chosen", [P, E], F32)
    carry = sb("carry", [P, E], F32)
    carryb = sb("carryb", [P, E], BF16)
    over = sb("over", [P, SUB, E], F32)
    place = sb("place", [P, SUB, E], F32)
    pk = sb("pk", [P, TOPK, SUB, E], F32)
    destf = sb("destf", [P, TOPK * SUB], F32)
    tok = sb("tok", [P, SUB], I32)

    with ExitStack() as pre:
        psb = lambda name, shape, dt: pre.enter_context(nc.sbuf_tensor(name, shape, dt))
        wkv = psb("wkv", [P, 2, KC, D], F32)
        cx = psb("cx", [P, KC, B * S], F32)
        bv_row = psb("bv_row", [P, D], F32)
        kf = ou[:, :, 0:B * S]
        kh = psb("kh", [P, 2, B * S], F32R)
        kl = psb("kl", [P, 2, B * S], F32R)
        kbh = psb("kbh", [P, B, 2, 8 * S], F32R)
        kbl = psb("kbl", [P, B, 2, 8 * S], F32R)
    c_names = """tables ctx wk ident cst wq rest small k v kf kh kl vf fill kbh kbl hot ones_set
        k_first k_first_low v_first diag kept kept_low""".split()
    cs = {n: sem("c_" + n) for n in c_names}

    with ExitStack() as start:
        block = start.enter_context(nc.Block())
        counts = [*s.values(), *q_stacked, *whole["e"].values(), whole["s_w"], *whole["tok_in"], *row_stored]

        @block.sync
        def _(sp):
            sp.dma_start(cx[:], ctxT).then_inc(cs["ctx"], 16)
            sp.dma_start(cc[:, 0:P], cst[:, 0:P]).then_inc(cs["ident"], 16)

        @block.scalar
        def _(act):
            act.dma_start(wkv[:], watt[:, 0:2]).then_inc(cs["wk"], 16)
            act.dma_start(bc[:], bcols).then_inc(cs["wk"], 16)
            act.dma_start(bv_row[:], brows[0:1, :].to_broadcast([P, D])).then_inc(cs["wk"], 16)

            prime(act, counts[4::5])
            act.wait_ge(cs["fill"], 2)
            act.activation(ex[:], half[:], ACT.Exp).then_inc(cs["tables"], 1)

        @block.tensor
        def _(pe):
            prime(pe, counts[0::5] + counts[1::5])

        @block.vector
        def _(dve):
            prime(dve, counts[2::5] + counts[3::5])

        @block.gpsimd
        def _(pool):
            pool.memset(nobody[:], int(BIG)).then_inc(cs["fill"], 1)
            pool.memset(half[:], -0.5).then_inc(cs["fill"], 1)

    xr = sb("xr", [P, SUB, D], F32)
    rd = sb("rd", [P, CH], F32)
    ot = sb("ot", [P, 2, CH], F32)
    x1 = sb("x1", [P, SUB, D], F32)
    x2t = sb("x2t", [P, KC, CH], F32)

    QS = 16 * 19
    xv = x.rearrange("(c i p) d -> c p i d", i=SUB, p=P)
    ov = out.rearrange("(c i p) d -> c p i d", i=SUB, p=P)
    rv = rows.rearrange("(c i p) d -> c p i d", i=SUB, p=P)
    SC, PV = banks[4:6], banks[6:8]

    def steps(eng, step):
        for k in (-2, -1, 0):
            step(eng, k, k % 2, k // 2, True, k >= -1, k >= 0, False)
        with eng.Fori(0, NCH // 2 - 2) as b:
            step(eng, 2 * b + 1, 1, b, True, True, True, True)
            step(eng, 2 * b + 2, 0, b + 1, True, True, True, True)
        for k in range(NCH - 3, NCH + 1):
            step(eng, k, k % 2, k // 2, k < NCH - 2, k < NCH - 1, k < NCH, True)

    def bcast(ap, shape):
        return ap.to_broadcast(shape)

    with ExitStack() as main:
        block = main.enter_context(nc.Block())
        blk = cc[:, C_BLK:C_BLK + 616].rearrange("p (h s) -> p h s", h=8)

        def diagonal(eng, dst, src, b, m, ready):
            eng.tensor_tensor(dst[:, b, m, :].rearrange("p (h s) -> p h s", h=8),
                              src[:, m, b * S:b * S + S].rearrange("p (a s) -> p a s", a=1).to_broadcast([P, 8, S]),
                              blk, ALU.mult).then_inc(ready, 1)

        def first_keys(eng, r, part, loaded):
            for m in range(2):
                for t in range(3):
                    p0, lo = 64 * m + HD * t, GROWS * m + TO[t]
                    eng.dma_start(kst[r:r + 32, 3 * m + t:NT:6, 0:TL[t]].bitcast(F32),
                                  part[p0:p0 + 32, 0, :, lo:lo + TL[t]].bitcast(F32)).then_inc(loaded, 16)

        def keep_keys(eng, r, part, kept):
            for m in range(2):
                for t in range(3):
                    p0, lo = 64 * m + HD * t, GROWS * m + TO[t]
                    for side in range(2):
                        tile = 3 * m + t + 6 * side
                        eng.dma_start(k_tiles[1:B, r:r + 32, tile, 0:TL[t]].rearrange("b r c -> r b c"),
                                      part[p0:p0 + 32, 1:B, side, lo:lo + TL[t]].bitcast(F32)).then_inc(kept, 16)

        def values(eng, n, side, loaded):
            t0, g0 = 6 * side, 2 * side
            for hl, t, p0, s0, z in segments():
                src = vf[s0:s0 + z, bass.ds(n, 1), 64 * g0:64 * g0 + 128].rearrange("p a (g w) -> p (a g) w", g=2)
                eng.dma_start(vst[p0:p0 + z, t0 + t:t0 + 6:3, HD * hl:HD * hl + HD],
                              src[:, :, HD * hl:HD * hl + HD]).then_inc(loaded, 16)

        def sync_context(sp):
            sp.dma_start(wq[:], watt[:, 2]).then_inc(cs["wq"], 16)
            sp.dma_start(cc[:, P:C_N], cst[:, P:C_N]).then_inc(cs["cst"], 16)
            for dst, src in ((wo[:], watt[:, 3]), (wgs[:], wg), (bo_row[:], brows[1:2, :].to_broadcast([P, D]))):
                sp.dma_start(dst, src).then_inc(cs["rest"], 16)
            sp.wait_ge(cs["kbh"], 2)
            sp.dma_start(kbm[:].bitcast(F32), kbh[:, 0].bitcast(F32)).then_inc(s["kbm_loaded"], 16)
            for r in (0, 64):
                first_keys(sp, r, kbh, cs["k_first"])

        def pe_context(pe):
            pe.wait_ge(cs["ctx"], 16)
            pe.wait_ge(cs["wk"], 48)
            for m in range(2):
                for kc in range(KC):
                    mm = pe.matmul(banks[m][:, 0:B * S], wkv[:, 0, kc, P * m:P * m + P], cx[:, kc, :],
                                   start=(kc == 0), stop=(kc == KC - 1))
                mm.then_inc(cs["k"], 1)

        def pe_context_values(pe):
            for b in range(B):
                for kc in range(KC):
                    mm = pe.matmul(banks[4 + b][0:S, 0:D], cx[:, kc, b * S:b * S + S], wkv[:, 1, kc, :],
                                   start=(kc == 0), stop=(kc == KC - 1))
                mm.then_inc(cs["v"], 1)

        def act_context(act):
            act.wait_ge(cs["cst"], 16)
            act.activation(kst[96:112, :, :], cc[96:112, C_OH:C_OH + NT * TW].rearrange("p (t w) -> p t w", t=NT),
                           ACT.Copy).then_inc(cs["hot"], 1)
            for g in range(NG):
                act.activation(vst[:, 3 * g:3 * g + 3, :],
                               cc[0:TW, C_ON:C_ON + 3 * P].rearrange("p (j w) -> p j w", j=3), ACT.Copy)\
                   .then_inc(cs["ones_set"], 1)
            act.activation(tri[:], cc[:, C_TRI:C_TRI + P], ACT.Copy).then_inc(cs["small"], 1)

        def dve_context(dve):
            for m in range(2):
                dve.wait_ge(cs["k"], m + 1)
                dve.tensor_scalar(kf[:, m, :], banks[m][:, 0:B * S], bc[:, 1, m:m + 1], None, ALU.add)\
                   .then_inc(cs["kf"], 1)
                dve.wait_ge(cs["kf"], m + 1)
                dve.tensor_copy(kh[:, m, :], kf[:, m, :]).then_inc(cs["kh"], 1)
                dve.wait_ge(cs["kh"], m + 1)
                dve.tensor_tensor(kl[:, m, :], kf[:, m, :], kh[:, m, :], ALU.subtract).then_inc(cs["kl"], 1)
            dve.wait_ge(cs["cst"], 16)
            for m in range(2):
                diagonal(dve, kbh, kh, 0, m, cs["kbh"])
            for b in range(B):
                dve.wait_ge(cs["v"], b + 1)
                dve.tensor_tensor(vf[:, b, :], banks[4 + b][0:S, 0:D], bv_row[0:S, :], ALU.add).then_inc(cs["vf"], 1)

        def dve_context_rest(dve):
            for b in range(1, B):
                for m in range(2):
                    diagonal(dve, kbh, kh, b, m, cs["kbh"])
            for b in range(1, B):
                for m in range(2):
                    diagonal(dve, kbl, kl, b, m, cs["kbl"])
            dve.memset(ones[:], 1.0).then_inc(cs["small"], 1)
            dve.tensor_copy(carry[:], cc[:, C_START:C_START + E]).then_inc(s["carry_ready"], 1)
            dve.wait_ge(s["carry_ready"], after(1))
            dve.tensor_copy(carryb[:], carry[:]).then_inc(s["carryb_ready"], 1)

        def pool_context(pool):
            pool.wait_ge(cs["fill"], 2)
            table = slot_token.rearrange("(p n) o -> p (n o)", p=32)
            for i in range(2):
                pool.dma_start(table[16 * i:16 * i + 16], nobody[16 * i:16 * i + 16]).then_inc(s_scat[i], 16)
            pool.wait_ge(cs["cst"], 16)
            pool.wait_ge(cs["kl"], 2)
            for m in range(2):
                diagonal(pool, kbl, kl, 0, m, cs["kbl"])
            pool.wait_ge(cs["kbl"], 2)
            first_keys(pool, 32, kbl, cs["k_first_low"])
            pool.wait_ge(cs["vf"], B)
            pool.wait_ge(cs["ones_set"], NG)
            values(pool, 0, 0, cs["v_first"])
            pool.iota(tok[:], pattern=[[P, SUB]], base=0, channel_multiplier=1).then_inc(s["tok_ready"], 1)
            pool.memset(number[:, 1], 0).then_inc(s["pool_set"], 1)
            pool.memset(dest[:, 1], int(BIG)).then_inc(s["pool_set"], 1)

        def sync_step(sp, k, u, n, ln_on, a_on, b_on, f_on):
            a, j, v = k + 1, k - 1, 1 - u
            if f_on:
                sp.wait_ge(s["x1_ready"], after(SUB * j))
                sp.dma_start(xr[:], xv[j]).then_inc(s["xr_loaded"], 16)
            if not b_on and f_on:
                sp.dma_start(whole["w1raw"][:], w1[0]).then_inc(whole["s_w"], 16)
                sp.dma_start(whole["w2raw"][:], w2[0]).then_inc(whole["s_w"], 16)
            if ln_on:
                sp.wait_ge(s["xn_ready"], after(SUB * (a + 1)))
                sp.dma_start(xt[:], xv[a + 1]).then_inc(s["x_loaded"], 16)
            if ln_on and not a_on:
                sync_context(sp)
            if a_on and b_on and u == 1:
                sp.wait_ge(cs["diag"], 16 * (B - 1))
                sp.wait_ge(s["max_psum"], after(SUB * NG * a))
                sp.dma_start(kbm[:].bitcast(F32).rearrange("p m c -> p (m c)"), k_diag[n + 1])\
                  .then_inc(s["kbm_loaded"], 16)
            if b_on and f_on and u == 0:
                stationary(sp, k, n, 1)
            if a_on:
                sp.wait_ge(s["q_lo"], after(2 * (a + 1)))
                sp.wait_ge(s["sc_psum"], after(NT * k))
                for m in range(2):
                    for t in range(3):
                        p0, at = 64 * m + HD * t, 2 * (3 * m + t)
                        for r, src in ((0, qh), (32, qh), (64, ql)):
                            sp.dma_start(qs[r:r + 32, v, at:at + 2, :].bitcast(F32),
                                         src[p0:p0 + 32].bitcast(F32)).then_inc(q_stacked[v], 16)
            if f_on:
                sp.wait_ge(s["x1_ready"], after(SUB * (j + 1)))
                sp.dma_start(ov[j], x1[:]).then_inc(s["x1_stored"], 16)
            if a_on:
                sp.wait_ge(s["nmt_ready"], after(a + 1))
                sp.dma_start(qs[96:112, v, :, :].bitcast(F32),
                             bcast(nmt[:].bitcast(F32).rearrange("h (a c) -> h a c", a=1), [H, NT, CH]))\
                  .then_inc(q_stacked[v], 16)
            if a_on and u == 1:
                if b_on:
                    stationary(sp, a, n + 1, 0)
                else:
                    sp.wait_ge(cs["vf"], B)
                    sp.wait_ge(cs["ones_set"], NG)
                    values(sp, 0, 1, s["v_loaded1"])
                    sp.wait_ge(cs["kbh"], 2 * B)
                    sp.dma_start(k_diag[1].rearrange("p (m c) -> p m c", m=2), kbh[:, 1].bitcast(F32))\
                      .then_inc(cs["diag"], 16)
                    keep_keys(sp, 0, kbh, cs["kept"])
            if b_on and not f_on:
                for b in range(2, B):
                    sp.dma_start(k_diag[b].rearrange("p (m c) -> p m c", m=2), kbh[:, b].bitcast(F32))\
                      .then_inc(cs["diag"], 16)
                keep_keys(sp, 64, kbh, cs["kept"])

            if f_on:
                sp.wait_ge(s["gate_row"], after(j + 1))
                sp.dma_start(rv[j], row[:, v]).then_inc(row_stored[v], 16)

        def stationary(sp, c, n, half):
            t0 = 6 * half
            sp.wait_ge(cs["kept"], 16 * 24)
            sp.wait_ge(cs["kept_low"], 16 * 12)
            sp.wait_ge(s["sc_psum"], after(NT * (c - 1) + t0 + 6))
            for t in range(3):
                sp.dma_start(kst[0:96, t0 + t:t0 + 6:3, 0:TL[t]].bitcast(F32),
                             k_tiles[n, 0:96, t0 + t:t0 + 6:3, 0:TL[t]]).then_inc(s[f"k_loaded{half}"], 16)
            sp.wait_ge(s["pv_tile"], after(NT * (c - 1) + t0 + 6))
            values(sp, n, half, s[f"v_loaded{half}"])

        @block.sync
        def _(sp):
            steps(sp, sync_step)
            sp.wait_ge(s["x1_stored"], after(16 * NCH))

        def pe_scores(pe, k, u, n, t, first):
            if t == 0:
                pe.wait_ge(q_stacked[u], after(QS * (n + 1)))
            if first and t == 0:
                pe.wait_ge(cs["vf"], B)
                pe.wait_ge(cs["hot"], 1)
                pe.wait_ge(cs["k_first"], 16 * 12)
                pe.wait_ge(cs["k_first_low"], 16 * 6)
            if t in (0, 6):
                pe.wait_ge(s[f"k_loaded{t // 6}"], after(16 * 3 * n))
            pe.wait_ge(s["p_ready"], after(NT * k + t - 1))
            pe.matmul(SC[t % 2][0:TL[t % 3], :], kst[:, t, 0:TL[t % 3]], qs[:, u, 2 * (t % 6) + t // 6, :],
                      start=True, stop=True).then_inc(s["sc_psum"], 1)

        def pe_values(pe, k, n, t, first):
            g, w = t // 3, TL[t % 3]
            if t % 3 == 0:
                pe.wait_ge(s["ou_ready"], after(NG * k + g - 1))
            if first and t == 0:
                pe.wait_ge(cs["v_first"], 16 * 6)
            if t in (0, 6):
                pe.wait_ge(s[f"v_loaded{t // 6}"], after(16 * 6 * (n + t // 6)))
            pe.wait_ge(s["p_ready"], after(NT * k + t + 1))
            pe.matmul(PV[g % 2][:], vst[0:w, t, :], pr[0:w, t % NP, :], start=(t % 3 == 0), stop=(t % 3 == 2))\
              .then_inc(s["pv_tile"], 1)

        def pe_maxima(pe, a, ba, pair):
            for c in (2 * pair, 2 * pair + 1):
                i, g = c // NG, c % NG
                if c == 0:
                    pe.wait_ge(s["kbm_loaded"], after(16 * (ba + 1)))
                if c < 2:
                    pe.wait_ge(s["q_lo"], after(2 * (a + 1)))
                else:
                    pe.wait_ge(s["max_read"], after(SUB * NG * a + c - 1))
                pe.matmul(banks[2 + c % 2][:, 0:GROWS], qh[:, g // 2, P * i:P * i + P],
                          kbm[:, g // 2, GROWS * (g % 2):GROWS * (g % 2) + GROWS],
                          start=True, stop=True).then_inc(s["max_psum"], 1)

        def pe_step(pe, k, u, n, ln_on, a_on, b_on, f_on):
            a, j, v = k + 1, k - 1, 1 - u
            ba = n + 1 if u == 1 else n
            for t in range(NT):
                if b_on:
                    pe_scores(pe, k, u, n, t, not f_on)
                if a_on and t in T_MAX:
                    pe_maxima(pe, a, ba, T_MAX.index(t))
                if b_on and t >= 2:
                    pe_values(pe, k, n, t - 2, not f_on)
                if a_on and T_MAX.count(t) == 2:
                    pe_maxima(pe, a, ba, T_MAX.index(t) + 1)
                if a_on and t == T_Q:
                    if not b_on:
                        pe.wait_ge(cs["wq"], 16)
                    pe.wait_ge(s["xt_ready"], after(KC * (a + 1)))
                    for m in range(2):
                        for kc in range(KC):
                            mm = pe.matmul(banks[2 + m][:], wq[:, kc, P * m:P * m + P], xT[:, kc, :],
                                           start=(kc == 0), stop=(kc == KC - 1))
                        mm.then_inc(s["q_psum"], 1)
                if f_on and t == T_SPREAD:
                    pe.wait_ge(s["rd_ready"], after(j + 1))
                    pe.wait_ge(s["over"], after(j))
                    pe.wait_ge(s["place"], after(j))
                    pe.wait_ge(cs["rest"], 48)
                    pe.wait_ge(cs["small"], 2)
                    for m in range(2):
                        pe.matmul(banks[m][:], cc[:, C_SEL + P * m:C_SEL + P * m + P], rd[:], start=True, stop=True)\
                          .then_inc(s["rb_psum"], 1)
                if f_on and t == T_WO:
                    for i in range(SUB):
                        for kc in range(KC):
                            pe.wait_ge(s["ot_ready"], after(2 * j + (kc + 1 if i == 0 else 2)))
                            mm = pe.matmul(banks[i // 2][:, D * (i % 2):D * (i % 2) + D],
                                           ot[:, kc, P * i:P * i + P], wo[:, kc, :],
                                           start=(kc == 0), stop=(kc == KC - 1))
                        if i % 2:
                            mm.then_inc(s["wo_psum"], 1)
                if f_on and t == T_X2T:
                    for i in range(SUB):
                        pe.wait_ge(s["x2_ready"], after(SUB * j + i + 1))
                        for h in range(KC):
                            mm = pe.transpose(banks[h][:, P * i:P * i + P], row[:, v, i, P * h:P * h + P], ident)
                            if i == SUB - 1:
                                mm.then_inc(s["x2t_psum"], 1)
                if f_on and t == T_LOGITS:
                    pe.wait_ge(s["x2t_ready"], after(KC * (j + 1)))
                    for i in range(SUB):
                        for kc in range(KC):
                            mm = pe.matmul(banks[0][:, E * i:E * i + E], x2t[:, kc, P * i:P * i + P], wgs[:, kc, :],
                                           start=(kc == 0), stop=(kc == KC - 1))
                    mm.then_inc(s["lg_psum"], 1)
                if a_on and t == T_NEGMAX:
                    pe.wait_ge(s["negmax"], after(a + 1))
                    for i in range(SUB):
                        mm = pe.transpose(banks[2][0:H, P * i:P * i + P], nm[:, i, :], ident)
                    mm.then_inc(s["nmt_psum"], 1)
                if f_on and t == T_POS:
                    pe.wait_ge(s["bothb_ready"], after(j + 1))
                    pe.wait_ge(s["carryb_ready"], after(j + 1))
                    for i in range(SUB):
                        o = banks[1][:, E * i:E * i + E]
                        pe.matmul(o, tri[:], bothb[:, i, :], start=True, stop=False)
                        for before in range(i):
                            pe.matmul(o, ones[:], bothb[:, before, :], start=False, stop=False)
                        mm = pe.matmul(o, ones[:], carryb[:], start=False, stop=True)
                    mm.then_inc(s["pos_psum"], 1)
            if ln_on and not a_on:
                pe.wait_ge(cs["ident"], 16)
            if ln_on:
                pe.wait_ge(s["nmt_ready"], after(a + 1))
                for i in range(SUB):
                    pe.wait_ge(s["xn_ready"], after(SUB * (a + 1) + i + 1))
                    for h in range(KC):
                        mm = pe.transpose(banks[2 + h][:, P * i:P * i + P], xn[:, i, P * h:P * h + P], ident)
                        if i == SUB - 1:
                            mm.then_inc(s["xt_psum"], 1)
            if ln_on and not a_on:
                pe_context_values(pe)
            if b_on:
                pe_values(pe, k, n, NT - 2, not f_on)
                pe_values(pe, k, n, NT - 1, not f_on)

        @block.tensor
        def _(pe):
            pe_context(pe)
            steps(pe, pe_step)

        def act_group(act, k, g):
            act.wait_ge(s["pv_tile"], after(NT * k + 3 * g + 3))
            act.wait_ge(s["rd_ready"], after(k))
            act.activation(dt[32 * g:32 * g + 32, :], PV[g % 2][64:96, :], ACT.Copy).then_inc(s["dt_ready"], 1)
            act.wait_ge(s["ot_ready"], after(2 * k))
            act.activation(ou[64 * (g % 2):64 * (g % 2) + 64, g // 2, :], PV[g % 2][0:64, :], ACT.Copy)\
               .then_inc(s["ou_ready"], 1)

        def act_step(act, k, u, n, ln_on, a_on, b_on, f_on):
            a, j, v = k + 1, k - 1, 1 - u
            for t in range(NT):
                if b_on:
                    w = TL[t % 3]
                    act.wait_ge(s["sc_psum"], after(NT * k + t + 1))
                    act.wait_ge(s["pv_tile"], after(NT * k + t - NP + 1))
                    act.activation(pr[0:w, t % NP, :], SC[t % 2][0:w, :], ACT.Exp, scale=SCALE)\
                       .then_inc(s["p_ready"], 1)
                    if t in (5, 8, 11):
                        act_group(act, k, (t - 5) // 3)
                if a_on and t == T_Q:
                    act.wait_ge(s["max_psum"], after(SUB * NG * a))
                    act.wait_ge(q_stacked[u], after(QS * (n + 1)))
                    for m in range(2):
                        act.wait_ge(s["q_psum"], after(2 * a + m + 1))
                        act.activation(qh[:, m, :], banks[2 + m][:], ACT.Identity, bias=bc[:, 0, m:m + 1])\
                           .then_inc(s["q_hi"], 1)
                if f_on and t == T_X2T:
                    act.wait_ge(s["lg_psum"], after(j))
                    for h in range(KC):
                        act.wait_ge(s["x2t_psum"], after(KC * j + h + 1))
                        act.activation(x2t[:, h, :], banks[h][:], ACT.Copy).then_inc(s["x2t_ready"], 1)
                if a_on and t == T_NEGMAX:
                    act.wait_ge(s["nmt_psum"], after(a + 1))
                    act.activation(nmt[:], banks[2][0:H, :], ACT.Copy).then_inc(s["nmt_ready"], 1)
                if f_on and t == T_EX:
                    act.wait_ge(s["dif_ready"], after(j + 1))
                    act.wait_ge(s["gate1"], after(j))
                    act.activation(ex[:], dif[:], ACT.Exp).then_inc(s["ex_ready"], 1)
            if ln_on:
                act.wait_ge(s["q_psum"], after(2 * (a + 1)))
                for h in range(KC):
                    act.wait_ge(s["xt_psum"], after(KC * (a + 1) + h + 1))
                    act.activation(xT[:, h, :], banks[2 + h][:], ACT.Copy).then_inc(s["xt_ready"], 1)
                if not a_on:
                    act_context(act)
            if b_on:
                act_group(act, k, NG - 1)

        @block.scalar
        def _(act):
            steps(act, act_step)

        def statistics(dve, src, c, stats, name, tiles):
            for i in tiles:
                if name == "x2":
                    dve.wait_ge(s["x1_ready"], after(SUB * c + i + 1))
                dve.wait_ge(s[name + "_mv"], after(SUB * c))
                dve.bn_stats(stats[:, i, :], src[:, i, :]).then_inc(s[name + "_stats"], 1)

        def aggregate(dve, c, stats, moments, name):
            dve.wait_ge(s[name + "_ready"], after(SUB * c))
            dve.wait_ge(s[name + "_stats"], after(SUB * (c + 1)))
            dve.sem_inc(passed["dve"], 1)
            for i in range(SUB):
                dve.bn_aggr(moments[:, i, :], stats[:, i, :]).then_inc(s[name + "_mv"], 1)

        def maxima(dve, a, pair):
            for c in (2 * pair, 2 * pair + 1):
                i, g = c // NG, c % NG
                dve.wait_ge(s["max_psum"], after(SUB * NG * a + c + 1))
                dve.tensor_reduce(mx[:, i, GH * g:GH * g + GH],
                                  banks[2 + c % 2][:, 0:GROWS].rearrange("p (h s) -> p h s", h=GH),
                                  AX_X, ALU.max).then_inc(s["max_read"], 1)

        def dve_step(dve, k, u, n, ln_on, a_on, b_on, f_on):
            a, j, v = k + 1, k - 1, 1 - u
            if f_on:
                dve.wait_ge(s["dt_ready"], after(NG * (j + 1)))
                dve.wait_ge(s["rb_psum"], after(2 * j))
                dve.reciprocal(rd[:], dt[:]).then_inc(s["rd_ready"], 1)
            if a_on:
                dve.wait_ge(q_stacked[u], after(QS * (n + 1)))
                for m in range(2):
                    dve.wait_ge(s["q_hi"], after(2 * a + m + 1))
                    dve.scalar_tensor_tensor(out=ql[:, m, :], in0=banks[2 + m][:], scalar=bc[:, 0, m:m + 1],
                                             in1=qh[:, m, :], op0=ALU.add, op1=ALU.subtract).then_inc(s["q_lo"], 1)
            if f_on:
                dve.wait_ge(s["ou_ready"], after(NG * (j + 1)))
                dve.wait_ge(s["wo_psum"], after(2 * j))
                for m in range(2):
                    dve.wait_ge(s["rb_psum"], after(2 * j + m + 1))
                    dve.tensor_tensor(ot[:, m, :], banks[m][:], ou[:, m, :], ALU.mult).then_inc(s["ot_ready"], 1)
            if a_on:
                dve.wait_ge(s["negmax"], after(a))
                maxima(dve, a, 0)
                maxima(dve, a, 1)
            if f_on:
                dve.wait_ge(s["xr_bias"], after(j + 1))
                dve.wait_ge(s["x1_stored"], after(16 * j))
                dve.wait_ge(s["x2_ready"], after(SUB * j))
                for m in range(2):
                    dve.wait_ge(s["wo_psum"], after(2 * j + m + 1))
                    for i in range(2 * m, 2 * m + 2):
                        dve.tensor_tensor(x1[:, i, :], banks[m][:, D * (i % 2):D * (i % 2) + D], xr[:, i, :],
                                          ALU.add).then_inc(s["x1_ready"], 1)
            for pair in range(2, 4):
                if a_on:
                    maxima(dve, a, pair)
                if f_on:
                    statistics(dve, x1, j, st2, "x2", range(2 * pair - 4, 2 * pair - 2))
            if f_on:
                aggregate(dve, j, st2, mv2, "x2")
            if a_on:
                for pair in range(4, 8):
                    maxima(dve, a, pair)
                dve.wait_ge(s["max_read"], after(SUB * NG * (a + 1)))
                dve.wait_ge(s["nmt_psum"], after(a))
                dve.tensor_scalar(nm[:], mx[:], -1.0, None, ALU.mult).then_inc(s["negmax"], 1)
            if f_on:
                dve.wait_ge(s["x2_rs"], after(j + 1))
                dve.wait_ge(s_scat[v], after(16 * SUB * TOPK * n, 16))
                dve.wait_ge(row_stored[v], after(16 * (n - 1) if u == 0 else 16 * n))
                for i in range(SUB):
                    dve.tensor_scalar(row[:, v, i, 0:D], x1[:, i, :], mv2[:, i, 0:1], rs2[:, i:i + 1],
                                      ALU.subtract, ALU.mult).then_inc(s["x2_ready"], 1)
                dve.wait_ge(s["tok_ready"], after(j + 1))
                dve.tensor_copy(number[:, v], tok[:]).then_inc(s["tok_row"], 1)
            if ln_on:
                dve.wait_ge(s["x_loaded"], after(16 * (a + 2)))
                statistics(dve, xt, a + 1, st, "xn", range(SUB))
                aggregate(dve, a + 1, st, mv, "xn")
            if f_on:
                dve.wait_ge(s["tok_row"], after(j + 1))
                dve.tensor_scalar(tok[:], tok[:], CH, None, ALU.add).then_inc(s["tok_ready"], 1)
                choose(dve, j)
            if ln_on:
                dve.wait_ge(s["xn_rs"], after(a + 2))
                dve.wait_ge(s["xt_psum"], after(KC * (a + 1)))
                for i in range(SUB):
                    dve.tensor_scalar(xn[:, i, :], xt[:, i, :], mv[:, i, 0:1], rs[:, i:i + 1],
                                      ALU.subtract, ALU.mult).then_inc(s["xn_ready"], 1)
                if not a_on:
                    dve_context(dve)
                elif not b_on:
                    dve_context_rest(dve)
            if f_on:
                route(dve, j, v)

        def choose(dve, j):
            dve.wait_ge(s["dif_ready"], after(j))
            dve.wait_ge(s["idx_ready"], after(SUB * j))
            dve.wait_ge(s["lg_psum"], after(j + 1))
            dve.sem_inc(passed["dve"], 1)
            for i in range(SUB):
                dve.max(top8[:, i, :], banks[0][:, E * i:E * i + E]).then_inc(s["top_ready"], 1)
            dve.wait_ge(s["idf_ready"], after(j))
            for i in range(SUB):
                dve.wait_ge(s["top_ready"], after(SUB * j + i + 1))
                dve.sem_inc(passed["dve"], 1)
                dve.max_index(idx8[:, i, :], top8[:, i, :], banks[0][:, E * i:E * i + E]).then_inc(s["idx_ready"], 1)
            dve.wait_ge(s["ex_ready"], after(j))
            dve.tensor_tensor(dif[:], top8[:, :, 1], top8[:, :, 0], ALU.subtract).then_inc(s["dif_ready"], 1)
            dve.wait_ge(s["idx_ready"], after(SUB * (j + 1)))
            dve.wait_ge(s["oh_ready"], after(j))
            dve.tensor_copy(idf[:], idx8[:, :, 0:TOPK].rearrange("p i r -> p r i")).then_inc(s["idf_ready"], 1)
            dve.wait_ge(s["idf_ready"], after(j + 1))
            dve.wait_ge(s["pk_ready"], after(j))
            dve.wait_ge(s["gw_ready"], after(j))
            dve.wait_ge(s["bothb_ready"], after(j))
            pairs = lambda ap: ap.rearrange("p r i -> p (r i)").rearrange("p (c a) -> p c a", a=1)
            flat = lambda ap: ap.rearrange("p r i e -> p (r i) e")
            dve.tensor_tensor(flat(oh[:]), cc[:, C_IO:C_IO + 64].rearrange("p (c e) -> p c e", e=E),
                              bcast(pairs(idf[:]), [P, TOPK * SUB, E]), ALU.is_equal).then_inc(s["oh_ready"], 1)
            dve.wait_ge(s["oh_ready"], after(j + 1))
            dve.wait_ge(s["pos_psum"], after(j))
            dve.wait_ge(s["chosen"], after(j))
            dve.tensor_tensor(bothb[:], oh[:, 0], oh[:, 1], ALU.add).then_inc(s["bothb_ready"], 1)

        def route(dve, j, v):
            pairs = lambda ap: ap.rearrange("p r i -> p (r i)").rearrange("p (c a) -> p c a", a=1)
            flat = lambda ap: ap.rearrange("p r i e -> p (r i) e")
            dve.wait_ge(s["ex_ready"], after(j + 1))
            dve.wait_ge(s["gate0"], after(j))
            dve.tensor_scalar(den[:], ex[:], 1.0, None, ALU.add).then_inc(s["den_ready"], 1)
            dve.wait_ge(s["bothb_ready"], after(j + 1))
            dve.wait_ge(s["carry_ready"], after(j + 1))
            dve.tensor_reduce(chosen[:], bothb[:].rearrange("p i e -> p e i"), AX_X, ALU.add).then_inc(s["chosen"], 1)
            dve.wait_ge(s["den_ready"], after(j + 1))
            dve.wait_ge(s["gw_ready"], after(j))
            dve.reciprocal(gate[:, 0], den[:]).then_inc(s["gate0"], 1)
            dve.wait_ge(s["chosen"], after(j + 1))
            dve.wait_ge(s["carryb_ready"], after(j + 1))
            dve.tensor_tensor(carry[:], carry[:], chosen[:], ALU.add).then_inc(s["carry_ready"], 1)
            dve.wait_ge(s["gate0"], after(j + 1))
            dve.tensor_tensor(gate[:, 1], gate[:, 0], ex[:], ALU.mult).then_inc(s["gate1"], 1)
            dve.wait_ge(s["gate1"], after(j + 1))
            dve.wait_ge(s["gate_row"], after(j))
            dve.tensor_tensor(flat(gw[:]), flat(oh[:]), bcast(pairs(gate[:]), [P, TOPK * SUB, E]), ALU.mult)\
               .then_inc(s["gw_ready"], 1)
            dve.wait_ge(s["pos_psum"], after(j + 1))
            dve.wait_ge(s["place"], after(j))
            ranks = banks[1][:, 0:SUB * E].rearrange("p (i e) -> p i e", e=E)
            dve.tensor_tensor(over[:], ranks, cc[:, C_EB:C_EB + 32].rearrange("p (i e) -> p i e", e=E),
                              ALU.is_ge).then_inc(s["over"], 1)
            dve.wait_ge(s["gw_ready"], after(j + 1))
            dve.tensor_tensor(row[:, v, :, D:ROW], gw[:, 0], gw[:, 1], ALU.add).then_inc(s["gate_row"], 1)
            dve.wait_ge(s["over"], after(j + 1))
            dve.wait_ge(s["pk_ready"], after(j))
            dve.scalar_tensor_tensor(out=place[:], in0=over[:], scalar=BIG, in1=ranks, op0=ALU.mult, op1=ALU.add)\
               .then_inc(s["place"], 1)
            dve.wait_ge(s["carry_ready"], after(j + 2))
            dve.tensor_copy(carryb[:], carry[:]).then_inc(s["carryb_ready"], 1)
            dve.wait_ge(s["place"], after(j + 1))
            dve.wait_ge(s["destf_ready"], after(j))
            dve.tensor_tensor(pk[:], oh[:], bcast(place[:].rearrange("p (a i) e -> p a i e", a=1), [P, TOPK, SUB, E]),
                              ALU.mult).then_inc(s["pk_ready"], 1)
            dve.wait_ge(s["pk_ready"], after(j + 1))
            dve.wait_ge(s["dest_ready"], after(j))
            dve.tensor_reduce(destf[:], flat(pk[:]), AX_X, ALU.add).then_inc(s["destf_ready"], 1)
            dve.wait_ge(s["destf_ready"], after(j + 1))
            dve.tensor_copy(dest[:, v].rearrange("p r i -> p (r i)"), destf[:]).then_inc(s["dest_ready"], 1)

        @block.vector
        def _(dve):
            steps(dve, dve_step)

        def pool_step(pool, k, u, n, ln_on, a_on, b_on, f_on):
            a, j = k + 1, k - 1
            if f_on:
                pool.wait_ge(s["xr_loaded"], after(16 * (j + 1)))
                pool.tensor_tensor(xr[:], xr[:], bcast(bo_row[:].rearrange("p (a d) -> p a d", a=1), [P, SUB, D]),
                                   ALU.add).then_inc(s["xr_bias"], 1)
                pool.wait_ge(s_scat[0], 16)
                pool.wait_ge(s_scat[1], 16)
                pool.wait_ge(s["pool_set"], after(2))
                pool.wait_ge(s["tok_row"], after(j))
                pool.wait_ge(s["dest_ready"], after(j))
                pool.sem_inc(passed["pool"], 1)
                for c in range(SUB * TOPK):
                    scatter(pool, whole, slot_token, u, c)
                variance_root(pool, j, mv2, ve2, rs2, "x2")
            if b_on and not a_on:
                part, every = TT // NX, b2[:, :].rearrange("(a e) d -> a e d", a=1)
                for c in range(NX):
                    pool.dma_start(whole["b2r"][part * c:part * c + part], every.to_broadcast([part, E, D]))\
                        .then_inc(whole["added"][c], 16)
            if ln_on:
                variance_root(pool, a + 1, mv, ve, rs, "xn")
                if not a_on:
                    pool_context(pool)
                elif not b_on:
                    pool.wait_ge(cs["kbl"], 2 * B)
                    keep_keys(pool, 32, kbl, cs["kept_low"])

        def variance_root(pool, c, moments, plus, root, name):
            pool.wait_ge(s[name + "_rs"], after(c))
            pool.wait_ge(s[name + "_mv"], after(SUB * (c + 1)))
            pool.sem_inc(passed["pool"], 1)
            pool.tensor_scalar(plus[:], moments[:, :, 1], EPS, None, ALU.add).then_inc(s[name + "_ve"], 1)
            pool.wait_ge(s[name + "_ve"], after(c + 1))
            pool.wait_ge(s[name + "_ready"], after(SUB * c))
            pool.tensor_tensor(root[:], plus[:], half[:], ALU.pow).then_inc(s[name + "_rs"], 1)

        @block.gpsimd
        def _(pool):
            steps(pool, pool_step)


def experts(nc, ctx, whole, passed, banks, slot_token, rows, w1, b1, w2, b2, out):
    sb = lambda name, shape, dt: ctx.enter_context(nc.sbuf_tensor(name, shape, dt))
    ident = whole["cc"][:, C_ID:C_ID + P]
    w1raw, w2raw, b2r = whole["w1raw"], whole["w2raw"], whole["b2r"]
    MT = HID // P
    sizes = [[min(TT, CAP - XC * c - TT * t) for t in range(3)] for c in range(NX)]
    STEPS = NX * MT
    assert all(min(z) > 64 and sum(z) % 2 == 0 for z in sizes)

    w1h = [sb(f"w1h{i}", [P, KC, HID], F32R) for i in range(2)]
    w1l = [sb(f"w1l{i}", [P, KC, HID], F32R) for i in range(2)]
    w2h = [sb(f"w2h{i}", [P, MT, D], F32R) for i in range(2)]
    w2l = [sb(f"w2l{i}", [P, MT, D], F32R) for i in range(2)]
    b1s = sb("b1s", [P, E, MT], F32)
    tkn = [sb(f"tkn{i}", [TT, 3], I32) for i in range(NX)]
    xin = [sb(f"xin{i}", [TT, 3, ROW], F32) for i in range(NX)]
    xh = sb("xh", [P, 2, KC, XC], F32R)
    xl = sb("xl", [P, 2, KC, XC], F32R)
    NH = 4
    hf = sb("hf", [P, NH, XC], F32)
    hh = sb("hh", [P, NH, XC], F32R)
    hl = sb("hl", [P, NH, XC], F32R)
    table_row = sb("table_row", [P, MT], F32)
    b2g = sb("b2g", [TT, 2, 3, D], F32)
    ys = sb("ys", [TT, 2, 3, D], F32)
    XT, HB, YB = banks[0:2], [banks[2], banks[3], banks[7]], banks[4:7]

    s, x_in, tok_in, added, s_w = whole["e"], whole["x_in"], whole["tok_in"], whole["added"], whole["s_w"]
    block = ctx.enter_context(nc.Block())

    def pairs(eng, turn):
        with eng.Fori(0, E // 2 - 1) as b:
            turn(eng, b, False)
        turn(eng, E // 2 - 1, True)

    def chunks(b, last):
        for eo in range(2):
            for c in range(NX):
                e = 2 * b + eo
                yield e, eo, c, NX * e + c, not (last and eo == 1 and c == NX - 1)

    def gate_of(e, c, t, z):
        return xin[c][0:z, t, bass.ds(D + e, 1)]

    def sync_pair(sp, b, last):
        for e, eo, c, q, _ in chunks(b, last):
            sp.wait_ge(added[c], after(48 * e, 16))
            lo, two, z = e * CAP + XC * c, 2 * TT, sizes[c][2]
            sp.dma_start(tkn[c][:, 0:2], slot_token[bass.ds(lo, two), :].rearrange("(t p) o -> p (t o)", p=TT),
                         allow_slow_non_contiguous=True).then_inc(tok_in[c], 16)
            sp.dma_start(tkn[c][0:z, 2:3], slot_token[bass.ds(lo + two, z), :]).then_inc(tok_in[c], 16)
            if c == 1 and not (last and eo == 1):
                sp.wait_ge(x_in[0], 48 * (e + 1))
                sp.wait_ge(s["w_split"], after(2 * (e + 1)))
                sp.dma_start(w1raw[:], w1[e + 1]).then_inc(s_w, 16)
                sp.dma_start(w2raw[:], w2[e + 1]).then_inc(s_w, 16)

    @block.sync
    def _(sp):
        sp.dma_start(b1s[:], b1).then_inc(s["b1_loaded"], 16)
        for u in range(2):
            sp.wait_ge(whole["s_scat"][u], after(16 * SUB * TOPK * (NCH // 2 + u), 16))
            sp.wait_ge(whole["row_stored"][u], after(16 * NCH // 2))
        pairs(sp, sync_pair)

    def transpose_x(pe, e, c, q):
        pe.wait_ge(x_in[c], 48 * (e + 1))
        for kc in range(KC):
            for t, z in enumerate(sizes[c]):
                mm = pe.transpose(XT[kc][:, TT * t:TT * t + z], xin[c][0:z, t, P * kc:P * kc + P], ident[0:z, 0:z])
            mm.then_inc(s["xt_psum"], 1)

    def layer1(pe, e, eo, c, q, m):
        n, at, g = sum(sizes[c]), MT * c + m, STEPS * e + MT * c + m
        o = HB[at % 3][:, 0:n]
        if m == 0:
            pe.wait_ge(s["xt_low"], after(KC * (q + 1)))
            if c == 0:
                pe.wait_ge(s["w_split"], after(2 * e + 1))
        if eo or at >= 3:
            pe.wait_ge(s["h_full"], after(g - 2))
        x0 = (NX * eo + c) % 2
        k = 0
        for w_, x_ in ((w1h, xh), (w1h, xl), (w1l, xh)):
            for kc in range(KC):
                mm = pe.matmul(o, w_[eo][:, kc, P * m:P * m + P], x_[:, x0, kc, 0:n], start=(k == 0), stop=(k == 5))
                k += 1
        mm.then_inc(s["h_psum"], 1)

    def layer2(pe, e, eo, c, q, m):
        g = STEPS * e + MT * c + m
        if m == 0:
            if c == 0:
                pe.wait_ge(s["w_split"], after(2 * e + 2))
        pe.wait_ge(s["h_low"], after(g + 1))
        for t, z in enumerate(sizes[c]):
            if m == 0:
                pe.wait_ge(s["y_ready"], after(3 * (q - 1) + t + 1 if eo or c else 3 * q))
            for h_, w_ in ((hh, w2h), (hh, w2l), (hl, w2h)):
                first, final = m == 0 and h_ is hh and w_ is w2h, m == MT - 1 and h_ is hl
                mm = pe.matmul(YB[t][0:z, 0:D], h_[:, m % NH, TT * t:TT * t + z], w_[eo][:, m, :],
                               start=first, stop=final)
        mm.then_inc(s["l2_done"], 1)

    def pe_pair(pe, b, last):
        behind = []
        for e, eo, c, q, follows in chunks(b, last):
            for m in range(MT):
                layer1(pe, e, eo, c, q, m)
                behind.append((e, eo, c, q, m))
                for _ in range(0 if m == 2 else 2 if m == 5 else 1):
                    if len(behind) > 2:
                        layer2(pe, *behind.pop(0))
                if m == 4 and follows:
                    transpose_x(pe, e + (c == NX - 1), (c + 1) % NX, q + 1)
        for one in behind:
            layer2(pe, *one)

    @block.tensor
    def _(pe):
        transpose_x(pe, 0, 0, 0)
        pairs(pe, pe_pair)

    def round_x(act, c, q, x0):
        n = sum(sizes[c])
        act.wait_ge(s["h_psum"], after(MT * (q - 1)))
        for kc in range(KC):
            act.wait_ge(s["xt_psum"], after(KC * q + kc + 1))
            act.activation(xh[:, x0, kc, 0:n], XT[kc][:, 0:n], ACT.Copy).then_inc(s["xt_high"], 1)

    def act_pair(act, b, last):
        for e, eo, c, q, follows in chunks(b, last):
            n = sum(sizes[c])
            for m in range(MT):
                at, g = MT * c + m, STEPS * e + MT * c + m
                act.wait_ge(s["l2_done"], after(STEPS * e if not eo and at < NH else g - NH + 1))
                act.wait_ge(s["h_psum"], after(g + 1))
                act.sem_inc(passed["act"], 1)
                for h_, ready in ((hh, "h_high"), (hf, "h_full")):
                    act.activation(h_[:, m % NH, 0:n], HB[at % 3][:, 0:n], ACT.Gelu_apprx_tanh,
                                   bias=b1s[:, e, m:m + 1]).then_inc(s[ready], 1)
                if m == 4 and follows:
                    round_x(act, (c + 1) % NX, q + 1, (NX * eo + c + 1) % 2)

    @block.scalar
    def _(act):
        act.wait_ge(s["b1_loaded"], after(16))
        act.activation(table_row[:], b1s[:, 0, :], ACT.Gelu_apprx_tanh).then_inc(s["table"], 1)
        round_x(act, 0, 0, 0)
        pairs(act, act_pair)

    def split_weights(dve, e, eo, part):
        raw, high, low = ((w1raw, w1h, w1l), (w2raw, w2h, w2l))[part // 2]
        if part % 2 == 0:
            dve.wait_ge(s_w, after(32 * (e + 1)))
            dve.wait_ge(s["l2_done"], after(STEPS * (e - 1)))
            dve.tensor_copy(high[eo][:], raw[:]).then_inc(s["w_high"], 1)
        else:
            dve.wait_ge(s["w_high"], after(2 * e + part // 2 + 1))
            dve.tensor_tensor(low[eo][:], raw[:], high[eo][:], ALU.subtract).then_inc(s["w_split"], 1)

    def rest_x(dve, c, q, x0):
        n = sum(sizes[c])
        for kc in range(KC):
            dve.wait_ge(s["xt_high"], after(KC * q + kc + 1))
            dve.tensor_tensor(xl[:, x0, kc, 0:n], XT[kc][:, 0:n], xh[:, x0, kc, 0:n], ALU.subtract)\
               .then_inc(s["xt_low"], 1)

    def outputs(dve, e, eo, c, q):
        y0 = (NX * eo + c) % 2
        dve.wait_ge(s["l2_done"], after(MT * (q + 1)))
        dve.wait_ge(s["b2g_ready"], after(3 * (q + 1)))
        if c >= 2:
            dve.wait_ge(added[c - 2], after(48 * (e + 1), 16))
        else:
            dve.wait_ge(added[c + 1], after(48 * e, 16))
        for t, z in enumerate(sizes[c]):
            dve.scalar_tensor_tensor(out=ys[0:z, y0, t, :], in0=YB[t][0:z, 0:D], scalar=gate_of(e, c, t, z),
                                     in1=b2g[0:z, y0, t, :], op0=ALU.mult, op1=ALU.add).then_inc(s["y_ready"], 1)

    def dve_pair(dve, b, last):
        behind = None
        for e, eo, c, q, follows in chunks(b, last):
            n = sum(sizes[c])
            for m in range(MT):
                g = STEPS * e + MT * c + m
                dve.wait_ge(s["h_full"], after(g + 1))
                dve.tensor_tensor(hl[:, m % NH, 0:n], hf[:, m % NH, 0:n], hh[:, m % NH, 0:n], ALU.subtract)\
                   .then_inc(s["h_low"], 1)
                if m == 1 and behind:
                    outputs(dve, *behind)
                if c == 1 and m % 2 and not (last and eo == 1):
                    split_weights(dve, e + 1, 1 - eo, m // 2)
                if m == 4 and follows:
                    rest_x(dve, (c + 1) % NX, q + 1, (NX * eo + c + 1) % 2)
            behind = (e, eo, c, q)
        outputs(dve, *behind)

    @block.vector
    def _(dve):
        for one in xin:
            dve.memset(one[:], 0.0).then_inc(s["x_clear"], 1)
        for part in range(4):
            split_weights(dve, 0, 0, part)
        rest_x(dve, 0, 0, 0)
        pairs(dve, dve_pair)

    def gather(pool, e, c):
        pool.wait_ge(tok_in[c], after(32 * (e + 1)))
        pool.sem_inc(passed["pool"], 1)
        for t, z in enumerate(sizes[c]):
            pool.indirect_dma_start(
                xin[c][0:z, t, :], None, rows[:, :],
                bass.IndirectOffsetOnAxis(ap=tkn[c][0:z, t:t + 1].bitcast(U32), axis=0),
                bounds_check=NTOK - 1, oob_is_err=False).then_inc(x_in[c], 16)

    def pool_pair(pool, b, last):
        for e, eo, c, q, _ in chunks(b, last):
            if not (last and eo == 1 and c > NX - 3):
                gather(pool, e + (c + 2) // NX, (c + 2) % NX)
            y0 = (NX * eo + c) % 2
            pool.wait_ge(s["y_ready"], after(3 * q))
            pool.wait_ge(x_in[c], 48 * (e + 1))
            pool.sem_inc(passed["pool"], 1)
            for t, z in enumerate(sizes[c]):
                pool.tensor_tensor(b2g[0:z, y0, t, :], b2r[0:z, e, :], gate_of(e, c, t, z).to_broadcast([z, D]),
                                   ALU.mult).then_inc(s["b2g_ready"], 1)
            for t, z in enumerate(sizes[c]):
                if t == 0 and c == 0:
                    for before in range(NX):
                        pool.wait_ge(added[before], after(48 * e, 16))
                pool.wait_ge(s["y_ready"], after(3 * q + t + 1))
                pool.sem_inc(passed["pool"], 1)
                pool.indirect_dma_start(
                    out[:, :], bass.IndirectOffsetOnAxis(ap=tkn[c][0:z, t:t + 1].bitcast(U32), axis=0),
                    ys[0:z, y0, t, :], None, bounds_check=NTOK - 1, oob_is_err=False,
                    compute_op=ALU.add).then_inc(added[c], 16)

    @block.gpsimd
    def _(pool):
        for c in range(SUB * TOPK):
            scatter(pool, whole, slot_token, (NCH - 1) % 2, c)
        pool.wait_ge(s["x_clear"], after(NX))
        for c in range(NX):
            pool.wait_ge(added[c], 16)
        for c in range(2):
            gather(pool, 0, c)
        pairs(pool, pool_pair)
        for c in range(NX):
            pool.wait_ge(added[c], after(48 * E, 16))


def kernel(**inputs):
    import numpy as np
    import concourse.bacc as bacc
    from concourse.bass_utils import run_bass_kernel_spmd

    a = {k: np.asarray(v) for k, v in inputs.items()}
    g = lambda name: a["L0_" + name]
    rows = lambda w: w.reshape(-1, P, w.shape[-1]).transpose(1, 0, 2)
    columns = lambda v: v.reshape(-1, P).T
    arrays = {
        "x": a["x"].reshape(NTOK, D),
        "ctxT": rows(a["ctx_1024"].reshape(B * S, D).T),
        "watt": np.stack([rows(g("xattn_W" + n)) for n in "kvqo"], axis=1),
        "wg": rows(g("ffn_Wg")),
        "bcols": np.stack([columns(g("xattn_b" + n)) for n in "qk"], axis=1),
        "brows": np.stack([g("xattn_bv"), g("xattn_bo")]),
        "w1": g("ffn_W1").reshape(E, KC, P, HID).transpose(0, 2, 1, 3),
        "b1": g("ffn_b1").reshape(E, HID // P, P).transpose(2, 0, 1),
        "w2": g("ffn_W2").reshape(E, HID // P, P, D).transpose(0, 2, 1, 3),
        "b2": g("ffn_b2"),
        "cst": constants(np),
    }
    arrays = {k: np.ascontiguousarray(v) for k, v in arrays.items()}
    nc = bacc.Bacc("TRN2", target_bir_lowering=False, num_devices=1)
    aps = {k: nc.dram_tensor(k, v.shape, F32, kind="ExternalInput").ap() for k, v in arrays.items()}
    out = nc.dram_tensor("out", (NTOK, D), F32, kind="ExternalOutput").ap()
    build(nc, out=out, **aps)
    r = run_bass_kernel_spmd(nc, [arrays], core_ids=[0])
    return r.results[0]["out"].reshape(B, L, D)
```
